# Optimizing a Trainium2 kernel written in Bass

```python
import numpy as np
import jax
import jax.numpy as jnp

def _softmax(x, axis=-1):
    return jax.nn.softmax(x, axis=axis)

def _gelu(x):
    return jax.nn.gelu(x, approximate=True)

def _silu(x):
    return jax.nn.silu(x)

def _sigmoid(x):
    return jax.nn.sigmoid(x)

def _layernorm(x, axis=-1, eps=1e-05):
    m = jnp.mean(x, axis=axis, keepdims=True)
    v = jnp.var(x, axis=axis, keepdims=True)
    return (x - m) / jnp.sqrt(v + eps)

def _scatter_add(tgt, idx, src, axis=0):
    return tgt.at[idx].add(src)

def _segment_sum(src, seg, n):
    return jax.ops.segment_sum(src, seg, n)
kernel_name = 'mk_dlrm_tower_d1_rec_r8_2dbebb'

def setup_inputs(seed: int=0):
    np.random.seed(seed)
    _w = jnp.asarray

    def _rec_inputs():
        import jax
        import jax.numpy as jnp
        _tk = jax.random.key(seed)
        ids = jnp.stack([jax.random.randint(jax.random.fold_in(_tk, 200 + f), (2048,), 0, v, jnp.int32) for f, v in enumerate([12500, 1250, 125000, 1000, 1000, 12500, 1000, 1250, 12500, 125000, 1250, 12500, 1250, 12500, 1250, 1250, 1250, 125000, 1000, 12500, 1000, 1000, 12500, 1250, 12500, 1250])], axis=1)
        tbl_0 = 0.05 * jax.random.normal(jax.random.fold_in(_tk, 500 + 0), (12500, 64), jnp.float32)
        tbl_1 = 0.05 * jax.random.normal(jax.random.fold_in(_tk, 500 + 1), (1250, 64), jnp.float32)
        tbl_2 = 0.05 * jax.random.normal(jax.random.fold_in(_tk, 500 + 2), (125000, 64), jnp.float32)
        tbl_3 = 0.05 * jax.random.normal(jax.random.fold_in(_tk, 500 + 3), (1000, 64), jnp.float32)
        tbl_4 = 0.05 * jax.random.normal(jax.random.fold_in(_tk, 500 + 4), (1000, 64), jnp.float32)
        tbl_5 = 0.05 * jax.random.normal(jax.random.fold_in(_tk, 500 + 5), (12500, 64), jnp.float32)
        tbl_6 = 0.05 * jax.random.normal(jax.random.fold_in(_tk, 500 + 6), (1000, 64), jnp.float32)
        tbl_7 = 0.05 * jax.random.normal(jax.random.fold_in(_tk, 500 + 7), (1250, 64), jnp.float32)
        tbl_8 = 0.05 * jax.random.normal(jax.random.fold_in(_tk, 500 + 8), (12500, 64), jnp.float32)
        tbl_9 = 0.05 * jax.random.normal(jax.random.fold_in(_tk, 500 + 9), (125000, 64), jnp.float32)
        tbl_10 = 0.05 * jax.random.normal(jax.random.fold_in(_tk, 500 + 10), (1250, 64), jnp.float32)
        tbl_11 = 0.05 * jax.random.normal(jax.random.fold_in(_tk, 500 + 11), (12500, 64), jnp.float32)
        tbl_12 = 0.05 * jax.random.normal(jax.random.fold_in(_tk, 500 + 12), (1250, 64), jnp.float32)
        tbl_13 = 0.05 * jax.random.normal(jax.random.fold_in(_tk, 500 + 13), (12500, 64), jnp.float32)
        tbl_14 = 0.05 * jax.random.normal(jax.random.fold_in(_tk, 500 + 14), (1250, 64), jnp.float32)
        tbl_15 = 0.05 * jax.random.normal(jax.random.fold_in(_tk, 500 + 15), (1250, 64), jnp.float32)
        tbl_16 = 0.05 * jax.random.normal(jax.random.fold_in(_tk, 500 + 16), (1250, 64), jnp.float32)
        tbl_17 = 0.05 * jax.random.normal(jax.random.fold_in(_tk, 500 + 17), (125000, 64), jnp.float32)
        tbl_18 = 0.05 * jax.random.normal(jax.random.fold_in(_tk, 500 + 18), (1000, 64), jnp.float32)
        tbl_19 = 0.05 * jax.random.normal(jax.random.fold_in(_tk, 500 + 19), (12500, 64), jnp.float32)
        tbl_20 = 0.05 * jax.random.normal(jax.random.fold_in(_tk, 500 + 20), (1000, 64), jnp.float32)
        tbl_21 = 0.05 * jax.random.normal(jax.random.fold_in(_tk, 500 + 21), (1000, 64), jnp.float32)
        tbl_22 = 0.05 * jax.random.normal(jax.random.fold_in(_tk, 500 + 22), (12500, 64), jnp.float32)
        tbl_23 = 0.05 * jax.random.normal(jax.random.fold_in(_tk, 500 + 23), (1250, 64), jnp.float32)
        tbl_24 = 0.05 * jax.random.normal(jax.random.fold_in(_tk, 500 + 24), (12500, 64), jnp.float32)
        tbl_25 = 0.05 * jax.random.normal(jax.random.fold_in(_tk, 500 + 25), (1250, 64), jnp.float32)
        _rk = jax.random.fold_in(_tk, 7)
        r_dense_t = 7.22013e-05 + 1.00017 * jax.random.normal(jax.random.fold_in(_rk, 101), (2048, 256), jnp.float32)
        W_top1 = 0.0360844 * jax.random.normal(jax.random.fold_in(_tk, 801), (768, 512), jnp.float32)
        W_top2 = 0.0441942 * jax.random.normal(jax.random.fold_in(_tk, 802), (512, 256), jnp.float32)
        W_top3 = 0.0625 * jax.random.normal(jax.random.fold_in(_tk, 803), (256, 1), jnp.float32)
        b_top1 = jnp.zeros((512,), jnp.float32)
        b_top2 = jnp.zeros((256,), jnp.float32)
        return (r_dense_t, ids, tbl_0, tbl_1, tbl_2, tbl_3, tbl_4, tbl_5, tbl_6, tbl_7, tbl_8, tbl_9, tbl_10, tbl_11, tbl_12, tbl_13, tbl_14, tbl_15, tbl_16, tbl_17, tbl_18, tbl_19, tbl_20, tbl_21, tbl_22, tbl_23, tbl_24, tbl_25, W_top1, b_top1, W_top2, b_top2, W_top3)
    r_dense_t, ids, tbl_0, tbl_1, tbl_2, tbl_3, tbl_4, tbl_5, tbl_6, tbl_7, tbl_8, tbl_9, tbl_10, tbl_11, tbl_12, tbl_13, tbl_14, tbl_15, tbl_16, tbl_17, tbl_18, tbl_19, tbl_20, tbl_21, tbl_22, tbl_23, tbl_24, tbl_25, W_top1, b_top1, W_top2, b_top2, W_top3 = _rec_inputs()

    def _L0_rec_setup():
        import jax, jax.numpy as jnp
        import numpy as np
        EPS = 1e-05
        NI = 33
        TRIL_I, TRIL_J = np.tril_indices(NI, k=-1)

        def layer_norm(x, g, b):
            m = jnp.mean(x, axis=-1, keepdims=True)
            v = jnp.mean(jnp.square(x - m), axis=-1, keepdims=True)
            return (x - m) * jax.lax.rsqrt(v + EPS) * g + b
        key = jax.random.key(seed)
        ks = jax.random.split(key, 8)
        B, D_DENSE, N_SP, D_SP = (4096, 256, 26, 64)
        E, PROJ, MAXD, NFLAT = (128, 32, 512, 528)
        dense_t = jax.random.normal(ks[0], (B, D_DENSE), dtype=jnp.float32)
        sparse_t = jax.random.normal(ks[1], (B, N_SP, D_SP), dtype=jnp.float32)
        Wd = jax.random.normal(ks[2], (E, D_DENSE), dtype=jnp.float32) / np.sqrt(D_DENSE)
        Ws = jax.random.normal(ks[3], (E, D_SP), dtype=jnp.float32) / np.sqrt(D_SP)
        Wsi = jax.random.normal(ks[4], (PROJ, N_SP), dtype=jnp.float32) / np.sqrt(N_SP)
        Wl = jax.random.normal(ks[5], (MAXD, NFLAT), dtype=jnp.float32) / np.sqrt(NFLAT)
        gd = jnp.ones((E,), jnp.float32)
        bd = jnp.zeros((E,), jnp.float32)
        gs = jnp.ones((E,), jnp.float32)
        bs = jnp.zeros((E,), jnp.float32)
        gsi = jnp.ones((PROJ,), jnp.float32)
        bsi = jnp.zeros((PROJ,), jnp.float32)
        gl = jnp.ones((MAXD,), jnp.float32)
        bl = jnp.zeros((MAXD,), jnp.float32)
        return {'dense_t': dense_t, 'sparse_t': sparse_t, 'Wd': Wd, 'gd': gd, 'bd': bd, 'Ws': Ws, 'gs': gs, 'bs': bs, 'Wsi': Wsi, 'gsi': gsi, 'bsi': bsi, 'Wl': Wl, 'gl': gl, 'bl': bl, 'dims_in_use': 384}
    _L0_rec_all = _L0_rec_setup()
    _L0_rec_in = {k: v for k, v in _L0_rec_all.items() if k in ('Wd', 'gd', 'bd', 'Ws', 'gs', 'bs', 'Wsi', 'gsi', 'bsi', 'Wl', 'gl', 'bl')}
    del _L0_rec_all
    return {'r_dense_t': r_dense_t, 'ids': ids, 'tbl_0': tbl_0, 'tbl_1': tbl_1, 'tbl_2': tbl_2, 'tbl_3': tbl_3, 'tbl_4': tbl_4, 'tbl_5': tbl_5, 'tbl_6': tbl_6, 'tbl_7': tbl_7, 'tbl_8': tbl_8, 'tbl_9': tbl_9, 'tbl_10': tbl_10, 'tbl_11': tbl_11, 'tbl_12': tbl_12, 'tbl_13': tbl_13, 'tbl_14': tbl_14, 'tbl_15': tbl_15, 'tbl_16': tbl_16, 'tbl_17': tbl_17, 'tbl_18': tbl_18, 'tbl_19': tbl_19, 'tbl_20': tbl_20, 'tbl_21': tbl_21, 'tbl_22': tbl_22, 'tbl_23': tbl_23, 'tbl_24': tbl_24, 'tbl_25': tbl_25, 'W_top1': W_top1, 'b_top1': b_top1, 'W_top2': W_top2, 'b_top2': b_top2, 'W_top3': W_top3, 'L0_rec_Wd': _L0_rec_in['Wd'], 'L0_rec_gd': _L0_rec_in['gd'], 'L0_rec_bd': _L0_rec_in['bd'], 'L0_rec_Ws': _L0_rec_in['Ws'], 'L0_rec_gs': _L0_rec_in['gs'], 'L0_rec_bs': _L0_rec_in['bs'], 'L0_rec_Wsi': _L0_rec_in['Wsi'], 'L0_rec_gsi': _L0_rec_in['gsi'], 'L0_rec_bsi': _L0_rec_in['bsi'], 'L0_rec_Wl': _L0_rec_in['Wl'], 'L0_rec_gl': _L0_rec_in['gl'], 'L0_rec_bl': _L0_rec_in['bl']}

def reference(r_dense_t, ids, tbl_0, tbl_1, tbl_2, tbl_3, tbl_4, tbl_5, tbl_6, tbl_7, tbl_8, tbl_9, tbl_10, tbl_11, tbl_12, tbl_13, tbl_14, tbl_15, tbl_16, tbl_17, tbl_18, tbl_19, tbl_20, tbl_21, tbl_22, tbl_23, tbl_24, tbl_25, W_top1, b_top1, W_top2, b_top2, W_top3, L0_rec_Wd, L0_rec_gd, L0_rec_bd, L0_rec_Ws, L0_rec_gs, L0_rec_bs, L0_rec_Wsi, L0_rec_gsi, L0_rec_bsi, L0_rec_Wl, L0_rec_gl, L0_rec_bl):
    import jax
    import jax.numpy as jnp

    def _L0_rec_ref(dense_t, sparse_t, Wd, gd, bd, Ws, gs, bs, Wsi, gsi, bsi, Wl, gl, bl, dims_in_use):
        import jax, jax.numpy as jnp
        import numpy as np
        EPS = 1e-05
        NI = 33
        TRIL_I, TRIL_J = np.tril_indices(NI, k=-1)

        def layer_norm(x, g, b):
            m = jnp.mean(x, axis=-1, keepdims=True)
            v = jnp.mean(jnp.square(x - m), axis=-1, keepdims=True)
            return (x - m) * jax.lax.rsqrt(v + EPS) * g + b
        x = layer_norm(dense_t @ Wd.T, gd, bd)
        y = layer_norm(jnp.einsum('bnd,ed->bne', sparse_t, Ws), gs, bs)
        y = jnp.einsum('bne,pn->bep', y, Wsi)
        y = layer_norm(y, gsi, bsi)
        y = jnp.swapaxes(y, 1, 2)
        T = jnp.concatenate([x[:, None, :], y], axis=1)
        Z = jnp.einsum('bnd,bmd->bnm', T, T)
        Zflat = Z[:, TRIL_I, TRIL_J]
        out = layer_norm(Zflat @ Wl.T, gl, bl)
        maxd = out.shape[-1]
        mask = (jnp.arange(maxd) < dims_in_use).astype(out.dtype)
        return out * mask
    e = jnp.stack([tbl_0[ids[:, 0]], tbl_1[ids[:, 1]], tbl_2[ids[:, 2]], tbl_3[ids[:, 3]], tbl_4[ids[:, 4]], tbl_5[ids[:, 5]], tbl_6[ids[:, 6]], tbl_7[ids[:, 7]], tbl_8[ids[:, 8]], tbl_9[ids[:, 9]], tbl_10[ids[:, 10]], tbl_11[ids[:, 11]], tbl_12[ids[:, 12]], tbl_13[ids[:, 13]], tbl_14[ids[:, 14]], tbl_15[ids[:, 15]], tbl_16[ids[:, 16]], tbl_17[ids[:, 17]], tbl_18[ids[:, 18]], tbl_19[ids[:, 19]], tbl_20[ids[:, 20]], tbl_21[ids[:, 21]], tbl_22[ids[:, 22]], tbl_23[ids[:, 23]], tbl_24[ids[:, 24]], tbl_25[ids[:, 25]]], axis=1)
    z = _L0_rec_ref(r_dense_t, e, L0_rec_Wd, L0_rec_gd, L0_rec_bd, L0_rec_Ws, L0_rec_gs, L0_rec_bs, L0_rec_Wsi, L0_rec_gsi, L0_rec_bsi, L0_rec_Wl, L0_rec_gl, L0_rec_bl, 384)
    z = z.reshape(z.shape[0], -1)
    h = jnp.concatenate([z, r_dense_t], axis=1)
    h = jnp.maximum(h @ W_top1 + b_top1, 0.0)
    h = jnp.maximum(h @ W_top2 + b_top2, 0.0)
    y = h @ W_top3
    return y

_drawn_inputs = setup_inputs


def setup_inputs(seed=0):
    import zlib

    import numpy as np

    out = dict(_drawn_inputs(seed))
    spreads = {'b_top1': (0.0, 0.1),
     'b_top2': (0.0, 0.1),
     'L0_rec_gd': (1.0, 0.6),
     'L0_rec_bd': (0.0, 0.8),
     'L0_rec_gs': (1.0, 0.6),
     'L0_rec_bs': (0.0, 0.1),
     'L0_rec_gsi': (1.0, 0.2),
     'L0_rec_bsi': (0.0, 0.1),
     'L0_rec_gl': (1.0, 0.2),
     'L0_rec_bl': (0.0, 0.1)}
    factors = {}
    for name, (base, spread) in spreads.items():
        noise = np.random.default_rng([zlib.crc32(name.encode()), seed]).standard_normal(out[name].shape)
        drawn = base * np.exp(spread * noise) if base else spread * noise
        out[name] = jnp.asarray(drawn.astype(out[name].dtype))
    for name, factor in factors.items():
        out[name] = (out[name] * factor).astype(out[name].dtype)
    return out
```

```python
from contextlib import ExitStack

import numpy as np
import concourse.bass as bass
from concourse import mybir

F32 = mybir.dt.float32
F32R = mybir.dt.float32r
I32 = mybir.dt.int32
ALU = mybir.AluOpType
ACT = mybir.ActivationFunctionType
AX = mybir.AxisListType

P = 128
NF = 26
DS = 64
E = 128
PJ = 32
DD = 256
KOUT = 512
KUSE = 384
H1, H2 = 512, 256
EPS = 1e-5
BATCH = 2048
SUPERS = 4
ITERS = 4
SUPER = BATCH // SUPERS
GROUP = 64
TILES = GROUP * NF // P
CHUNKS = [(0, 4), (4, 7), (7, 10), (10, 13)]
STEPS = ITERS * len(CHUNKS)
BS = GROUP // 4
QC = PJ + 2
TW = 4 * PJ + 8
NG = PJ // 4
OFF = [sum(4 * (4 * h + 3) for h in range(g)) for g in range(NG + 1)]
XOFF, ROFF, SXOFF, ONEOFF = OFF[NG], OFF[NG] + PJ, OFF[NG] + 2 * PJ, OFF[NG] + 2 * PJ + 1
FCH = 5
FEAT = FCH * P
WINDOW = 6


def first_sample(i):
    return P * i // NF


def last_sample(i):
    return (P * i + P - 1) // NF


def u_pieces(k):
    out = []
    for i in range(TILES):
        a, b = max(first_sample(i), BS * k), min(last_sample(i) + 1, BS * (k + 1))
        if a < b:
            out.append((i, a, b))
    return out


def build(nc, a, out):
    ctx = ExitStack()
    with ctx:
        def sb(name, shape, dt=F32):
            return ctx.enter_context(nc.sbuf_tensor(name, shape, dt))

        def sem(name):
            return ctx.enter_context(nc.semaphore(name))

        bank = [ctx.enter_context(nc.psum_tensor(f"bank{i}", [P, 512], F32)) for i in range(5)]
        bank_z = ctx.enter_context(nc.psum_tensor("bank_z", [P, 2, 512], F32))
        bank += [bank_z[:, 0, :], bank_z[:, 1, :]]
        bank.append(ctx.enter_context(nc.psum_tensor("bank7", [P, 512], F32)))
        ps_tr, ps_t, ps_u, ps_y = bank[0], bank[1], bank[2], [bank[3], bank[4]]
        ps_x = bank[7]

        ident = sb("ident", [P, P])
        center_p = sb("center_p", [PJ, PJ])
        window = sb("window", [P, TILES, WINDOW])
        ind_p = sb("ind_p", [P, FCH, QC])
        ind_q = sb("ind_q", [P, FCH, QC])
        ones = sb("ones", [P, P])
        eps = sb("eps", [P, 1])
        ws = sb("ws", [P, DS])
        wd = sb("wd", [P, DD])
        wsi = sb("wsi", [PJ, NF])
        gs, gd, bd = sb("gs", [P, 1]), sb("gd", [P, 1]), sb("bd", [P, 1])
        bs4 = sb("bs4", [P, E])
        ga, gb = sb("ga", [P, FCH]), sb("gb", [P, FCH])
        ba, bb = sb("ba", [P, FCH]), sb("bb", [P, FCH])
        gr = sb("gr", [P, 1])
        gl, bl = sb("gl", [P, 3]), sb("bl", [P, 3])
        b1, b2, w3 = sb("b1", [P, 4]), sb("b2", [P, 2]), sb("w3", [P, 2])
        wsc2 = sb("wsc2", [P, 2, DS])
        wg2 = sb("wg2", [P, 2, DS])
        gram2 = sb("gram2", [P, P])
        wg_hi, wg_lo = sb("wg_hi", [P, E], F32R), sb("wg_lo", [P, E], F32R)
        wsit = sb("wsit", [NF, PJ])
        mix = sb("mix", [P, TILES, WINDOW, PJ])
        bs_st = sb("bs_st", [P, E], F32R)
        bs_mv = sb("bs_mv", [P, BS, PJ], F32R)
        wd_hi, wd_lo = sb("wd_hi", [P, 2, E], F32R), sb("wd_lo", [P, 2, E], F32R)
        wl_hi, wl_lo = sb("wl_hi", [P, FCH, KOUT], F32R), sb("wl_lo", [P, FCH, KOUT], F32R)
        w1_hi, w1_lo = sb("w1_hi", [P, 5, H1], F32R), sb("w1_lo", [P, 5, H1], F32R)
        w2_hi, w2_lo = sb("w2_hi", [P, 4, H2], F32R), sb("w2_lo", [P, 4, H2], F32R)
        b1z = sb("b1z", [P, 4])

        ids = sb("ids", [P, ITERS * SUPERS, 2, TILES], I32)
        base = sb("base", [P, TILES], I32)
        rows_now = [sb(f"rows_now{i}", [P, 2, TILES], I32) for i in range(ITERS)]
        emb = [sb(f"emb{i}", [P, TILES, 2, DS]) for i in range(2)]
        scaled = sb("scaled", [P, TILES, 2, DS])
        embt = sb("embt", [P, 2, 4 * P])
        prod = sb("prod", [P, 8, DS])
        var_s, std_s, rstd_s = sb("var_s", [P, 8]), sb("std_s", [P, 8]), sb("rstd_s", [P, 8])
        upair = sb("upair", [P, 2, 2, 512], F32R)
        ysq = sb("ysq", [P, 2, 512])
        var_y, std_y, rstd_y = sb("var_y", [P, 2, BS]), sb("std_y", [P, 2, BS]), sb("rstd_y", [P, 2, BS])
        tvec = sb("tvec", [P, 2, 2, 4, TW])
        gram, gram_x = sb("gram", [P, PJ, P]), sb("gram_x", [P, 8, P])

        dense = sb("dense", [P, 4, DD])
        d_hi, d_lo = sb("d_hi", [P, 2, 512], F32R), sb("d_lo", [P, 2, 512], F32R)
        xa, xb = sb("xa", [P, 512]), sb("xb", [P, 512])
        xt = sb("xt", [P, 4, P])
        feat = sb("feat", [P, 4, FEAT])
        f_hi, f_lo = sb("f_hi", [P, FCH, 512], F32R), sb("f_lo", [P, FCH, 512], F32R)
        stats, mv = sb("stats", [P, 4, 6]), sb("mv", [P, 4, 2])
        std_o, rstd_o, shift_o = sb("std_o", [P, 4]), sb("rstd_o", [P, 4]), sb("shift_o", [P, 4])
        zn = sb("zn", [P, 4, KUSE])
        yrow = sb("yrow", [1, 512])
        wl_raw = gram[:, 0:4 * FCH, :].rearrange("p (c a) b -> p c (a b)", c=FCH)
        bmat = gram[:, 4 * FCH:5 * FCH, :]
        w1_raw = feat[:].rearrange("p j f -> p (j f)").rearrange("p (c m) -> p c m", c=5)
        center, blockmask = xa[:, 0:P], xb[:, 0:P]
        w2_raw = zn[:].rearrange("p j k -> p (j k)")[:, 0:4 * H2].rearrange("p (c m) -> p c m", c=4)
        spread = scaled[0:NF].rearrange("p i g d -> p i (g d)")
        h1_hi, h1_lo = f_hi[:, 0:4, :], f_lo[:, 0:4, :]
        z_hi, z_lo = sb("z_hi", [P, 3, 512], F32R), sb("z_lo", [P, 3, 512], F32R)
        h2 = zn[:].rearrange("p j k -> p (j k)")[:, 0:2 * 512].rearrange("p (m b) -> p m b", m=2)
        h1f = [feat[:, m, 0:512] for m in range(4)]

        s_ids, s_const, s_dense, s_out = sem("ids_loaded"), sem("weights_loaded"), sem("dense_loaded"), sem("out_stored")
        s_idx, s_now = sem("row_numbers_ready"), sem("rows_now_ready")
        s_seen = sem("wait_carrier")
        s_row = [[sem(f"rows_landed_{b}_{i}") for i in range(TILES)] for b in range(2)]
        pp, dp, s_prep_chain = sem("prep_pe"), sem("prep_dve"), sem("prep_chain")
        s_tr, s_t, s_u, s_y, s_z = sem("embt_done"), sem("t_done"), sem("u_done"), sem("y_done"), sem("gram_done")
        s_dt, s_xp, s_xv = sem("dense_turned"), sem("x_product"), sem("x_variance")
        s_q, s_sx, s_ft, s_o = sem("gram_turned"), sem("sum_x_done"), sem("feat_turned"), sem("block_out")
        s_zt, s_h1, s_h2, s_yo = sem("z_turned"), sem("h1_product"), sem("h2_product"), sem("y_product")
        s_yfree = sem("y_row_free")
        a_tr, a_std, a_hi, a_sq, a_sdy, a_z = (sem("embt_copied"), sem("std_s_ready"), sem("u_high"), sem("y_squared"),
                                               sem("std_y_ready"), sem("gram_copied"))
        a_dh, a_xs, a_xd = sem("dense_high"), sem("x_squared"), sem("std_x_ready")
        a_f, a_fh, a_sdo, a_zn, a_zh = (sem("feat_by_act"), sem("feat_high"), sem("std_o_ready"), sem("z_ready"),
                                        sem("z_high"))
        a_h1, a_h2, a_yo = sem("h1_ready"), sem("h2_ready"), sem("y_row_ready")
        d_prod, d_var, d_rs, d_sc, d_lo_u = (sem("t_times_s"), sem("var_s_ready"), sem("rstd_s_ready"),
                                             sem("rows_scaled"), sem("u_low"))
        d_vy, d_ry, d_t, d_x = sem("var_y_ready"), sem("rstd_y_ready"), sem("tvec_ready"), sem("x_in_tvec")
        d_dl, d_xr, d_xn, d_xt = sem("dense_low"), sem("rstd_x_ready"), sem("x_normed"), sem("xt_ready")
        d_f, d_fl, d_bn, d_ag, d_ro, d_sh, d_zl = (sem("feat_by_dve"), sem("feat_low"), sem("stats_ready"),
                                                   sem("mean_var_ready"), sem("rstd_o_ready"), sem("shift_o_ready"),
                                                   sem("z_low"))
        d_h1h, d_h1l = sem("h1_high"), sem("h1_low")

        block = ctx.enter_context(nc.Block())
        loads = [(ident, "c_ident"), (center, "c_center"), (blockmask, "c_blockmask"), (center_p, "c_center_p"),
                 (spread, "c_spread"), (window, "c_window"), (ind_p, "c_ind_p"), (ind_q, "c_ind_q"),
                 (ws, "Ws"), (wd, "Wd"), (wsi, "Wsi"), (gs, "gs"), (gd, "gd"), (bd, "bd"),
                 (ga, "ga"), (gb, "gb"), (ba, "ba"), (bb, "bb"), (gr, "gr"), (gl, "gl"), (bl, "bl"),
                 (b1, "b1"), (b2, "b2"), (w3, "w3")]
        NLOAD = len(loads) + 4 + 3

        def own_block(b, j):
            return b[:, 256 * (j % 2):256 * (j % 2 + 1)].rearrange("t (c j p) -> t c j p", c=2, j=4)[:, :, j, :]

        @block.sync
        def _(sp):
            sp.dma_start(ids[:], a["ids"]).then_inc(s_ids, 16)
            sp.dma_start(base[:], a["c_base"]).then_inc(s_ids, 16)
            for tile, name in loads:
                sp.dma_start(tile[:], a[name]).then_inc(s_const, 16)
            for k in range(4):
                sp.dma_start(bs4[32 * k:32 * k + 1, :], a["bs"]).then_inc(s_const, 16)
            sp.dma_start(wl_raw, a["Wl"]).then_inc(s_const, 16)
            sp.dma_start(w1_raw, a["W1"]).then_inc(s_const, 16)
            sp.dma_start(w2_raw, a["W2"]).then_inc(s_const, 16)

            def load_dense(s):
                sp.dma_start(dense[:], a["dense"][bass.ds(s * P, P), :, :]).then_inc(s_dense, 16)

            def store(s):
                sp.wait_ge(a_yo, s + 2)
                sp.dma_start(out[bass.ds(s, 1), :], yrow[0:1, :]).then_inc(s_out, 16)
                sp.wait_ge(s_out, 16 * s + 16)
                sp.sem_inc(s_yfree, 1)

            load_dense(0)
            with sp.Fori(0, SUPERS - 1) as s:
                sp.wait_ge(s_dt, s + 1)
                load_dense(s + 1)
                store(s)
            store(SUPERS - 1)

        @block.gpsimd
        def _(pool):
            pool.wait_ge(s_ids, 32)
            nc.gpsimd.tensor_tensor(ids[:].rearrange("p t g i -> p (t g) i"), ids[:].rearrange("p t g i -> p (t g) i"),
                                    base[:].unsqueeze(1).to_broadcast([P, 2 * ITERS * SUPERS, TILES]),
                                    ALU.add).then_inc(s_idx, 1)
            pool.wait_ge(s_idx, 1)
            with pool.Fori(0, SUPERS) as s:
                for it in range(ITERS):
                    b = it % 2
                    nc.gpsimd.tensor_copy(rows_now[it][:], ids[:, bass.ds(ITERS * s + it, 1), :, :].rearrange(
                        "p t g i -> p (t g) i")).then_inc(s_now, 1)
                    pool.wait_ge(s_now, ITERS * s + it + 1)
                    for c, (i0, i1) in enumerate(CHUNKS):
                        pool.wait_ge(d_sc, STEPS * s + 4 * it + c + 1)
                        pool.sem_inc(s_seen, 1)
                        for i in range(i0, i1):
                            for g in range(2):
                                nc.gpsimd.indirect_dma_start(
                                    emb[b][:, i, g, :], None, a["table"],
                                    bass.IndirectOffsetOnAxis(ap=rows_now[it][:, g, i:i + 1], axis=0),
                                ).then_inc(s_row[b][i], 16)

        def triple(pe, dst, terms, first=True, last=True):
            mm = None
            for n, (sh, sl, mh, ml) in enumerate(terms):
                for m, (x, y) in enumerate(((sh, mh), (sh, ml), (sl, mh))):
                    mm = pe.matmul(dst, x, y, start=first and n == 0 and m == 0,
                                   stop=last and n == len(terms) - 1 and m == 2)
            return mm

        @block.tensor
        def _(pe):
            pe.wait_ge(s_const, 16 * NLOAD)
            pe.matmul(bank[0][:, 0:DS], center[:], ws[:], start=True, stop=True)
            for c in range(2):
                pe.matmul(bank[1][:, c * E:(c + 1) * E], wd[:, c * P:(c + 1) * P], center[:], start=True, stop=True)
            pe.matmul(bank[2][0:NF, 0:PJ], wsi[:], center_p[:], start=True, stop=True).then_inc(pp, 1)
            pe.wait_ge(dp, 1)
            pe.matmul(bank[3][:, 0:P], wsc2[:].rearrange("p a d -> p (a d)"), wsc2[:].rearrange("p a d -> p (a d)"),
                      start=True, stop=True)
            pe.transpose(bank[4][:, 0:P], wg2[:].rearrange("p a d -> p (a d)"), ident[:])
            for i in range(TILES):
                pe.matmul(bank[5][:, i * PJ:(i + 1) * PJ], spread[:, i, :], wsit[:], start=True, stop=True)
            pe.matmul(bank[6][:, 0:PJ], ones[0:NF, :], wsit[:], start=True, stop=True)
            for c in range(FCH):
                pe.matmul(bank[7][:, :], bmat[:, c, :], wl_raw[:, c, :], start=(c == 0), stop=(c == FCH - 1))
            for m in range(4):
                for c in range(3):
                    mm = pe.matmul(bank[0][:, 256 + m:257 + m], w1_raw[:, c, m * P:(m + 1) * P], bl[:, c:c + 1],
                                   start=(c == 0), stop=(c == 2))
            mm.then_inc(pp, 1)
            pe.wait_ge(dp, 2)

            def turn_rows(s, n):
                it, c = divmod(n, 4)
                i0, i1 = CHUNKS[c]
                if n >= 1:
                    pe.wait_ge(a_tr, s * STEPS + n)
                for i in range(i0, i1):
                    pe.wait_ge(s_row[it % 2][i], 64 * s + 32 * (it // 2 + 1))
                    mm = pe.transpose(ps_tr[:, (i - i0) * P:(i - i0 + 1) * P],
                                      emb[it % 2][:, i, :, :].rearrange("p g d -> p (g d)"), ident[:])
                mm.then_inc(s_tr, 1)

            def times_gram(s, n):
                i0, i1 = CHUNKS[n % 4]
                pe.wait_ge(a_tr, s * STEPS + n + 1)
                if n >= 1:
                    pe.wait_ge(d_prod, s * STEPS + n)
                for i in range(i1 - i0):
                    mm = pe.matmul(ps_t[:, i * P:(i + 1) * P], embt[:, n % 2, i * P:(i + 1) * P], gram2[:],
                                   start=True, stop=True)
                mm.then_inc(s_t, 1)

            def mix_features(s, n):
                pe.wait_ge(d_sc, s * STEPS + 8 + n + 1)
                if n >= 1:
                    pe.wait_ge(d_lo_u, s * 2 * STEPS + 2 * n)
                if n == 0:
                    pe.wait_ge(a_yo, s + 1)
                k = n % 4
                pieces = u_pieces(k)
                for m, (i, x, y) in enumerate(pieces):
                    f = first_sample(i)
                    mm = pe.matmul(ps_u[:, (x - BS * k) * PJ:(y - BS * k) * PJ],
                                   scaled[:, i, :, :].rearrange("p g d -> p (g d)"),
                                   mix[:, i, x - f:y - f, :].rearrange("p s q -> p (s q)"),
                                   start=(m == 0), stop=(m == len(pieces) - 1), skip_group_check=True)
                mm.then_inc(s_u, 1)

            def project(s, n, g):
                pe.wait_ge(d_lo_u, s * 2 * STEPS + 2 * n + g + 1)
                if n >= 1:
                    pe.wait_ge(d_t, s * 2 * STEPS + 2 * n + g - 1)
                u = upair[:, n % 2, g, :]
                pe.matmul(ps_y[g][:, :], wg_hi[:], u, start=True, stop=False)
                pe.matmul(ps_y[g][:, :], wg_lo[:], u, start=False, stop=False)
                pe.matmul(ps_y[g][:, :], bs_st[:], bs_mv[:].rearrange("p s q -> p (s q)"),
                          start=False, stop=True).then_inc(s_y, 1)

            def gram_y(s, n, g):
                pe.wait_ge(d_x, s * STEPS + n + 1)
                pe.wait_ge(d_t, s * 2 * STEPS + 2 * n + g + 1)
                if n + g >= 1:
                    pe.wait_ge(a_z, s * 2 * STEPS + 2 * n + g)
                for t in range(4):
                    tv = tvec[:, n % 2, g, t, :]
                    mm = pe.matmul(bank_z[:, t // 2, (t % 2) * TW:(t % 2 + 1) * TW], tv[:, 0:4 * PJ], tv,
                                   start=True, stop=True)
                mm.then_inc(s_z, 1)

            def dense_turn(s):
                pe.wait_ge(s_dense, 16 * s + 16)
                for c in range(2):
                    for j in range(4):
                        mm = pe.transpose(bank[5 + c][:, j * P:(j + 1) * P], dense[:, j, c * P:(c + 1) * P], ident[:])
                mm.then_inc(s_dt, 1)

            def dense_product(s):
                pe.wait_ge(d_dl, 2 * s + 2)
                triple(pe, ps_x[:, :], [(wd_hi[:, c, :], wd_lo[:, c, :], d_hi[:, c, :], d_lo[:, c, :])
                                        for c in range(2)]).then_inc(s_xp, 1)

            def dense_variance(s):
                pe.wait_ge(a_xs, s + 1)
                pe.matmul(bank[5][:, :], ones[:], xa[:], start=True, stop=True).then_inc(s_xv, 1)

            def back(s):
                pe.wait_ge(a_z, (s + 1) * 2 * STEPS)
                for q in range(NG + 2):
                    if q >= 4:
                        pe.wait_ge([a_f, d_f][q % 2], (5 + q % 2) * s + (q - 4) // 2 + 1)
                    b = bank[[0, 1, 2, 7][q % 4]]
                    for m in range(4):
                        src = gram[:, 4 * q + m, :] if q < NG else gram_x[:, 4 * (q - NG) + m, :]
                        mm = pe.transpose(b[:, m * P:(m + 1) * P], src, ident[:])
                    mm.then_inc(s_q, 1)
                for j in range(4):
                    mm = pe.matmul(bank[3][:, j:j + 1], xt[:, j, :], ones[:, 0:1], start=True, stop=True)
                mm.then_inc(s_sx, 1)
                pe.wait_ge(a_f, 5 * s + 5)
                pe.wait_ge(d_f, 6 * s + 6)
                for c in range(FCH):
                    b = bank[[0, 1, 2, 7, 3][c]]
                    for j in range(4):
                        mm = pe.transpose(b[:, j * P:(j + 1) * P], feat[:, j, c * P:(c + 1) * P], ident[:])
                    mm.then_inc(s_ft, 1)
                for j in range(4):
                    b = bank[[4, 5, 6, 0][j]]
                    for c in range(FCH):
                        pe.wait_ge(d_fl, FCH * s + c + 1)
                        fh, fl = f_hi[:, c, j * P:(j + 1) * P], f_lo[:, c, j * P:(j + 1) * P]
                        mm = triple(pe, b[:, :], [(fh, fl, wl_hi[:, c, :], wl_lo[:, c, :])],
                                    first=(c == 0), last=(c == FCH - 1))
                    mm.then_inc(s_o, 1)
                for m in range(4):
                    if m >= 1:
                        pe.wait_ge(a_zn, 4 * s + m)
                    triple(pe, bank[3 + m][:, :],
                           [(w1_hi[:, 3 + c, m * P:(m + 1) * P], w1_lo[:, 3 + c, m * P:(m + 1) * P],
                             d_hi[:, c, :], d_lo[:, c, :]) for c in range(2)], last=False)
                    pe.wait_ge(a_zn, 4 * s + m + 1)
                    for c in range(3):
                        mm = pe.transpose(bank[[1, 2, 7][c]][:, m * P:(m + 1) * P], zn[:, m, c * P:(c + 1) * P], ident[:])
                mm.then_inc(s_zt, 1)
                for m in range(4):
                    for c in range(3):
                        pe.wait_ge(d_zl, 3 * s + c + 1)
                        mm = triple(pe, bank[3 + m][:, :],
                                    [(w1_hi[:, c, m * P:(m + 1) * P], w1_lo[:, c, m * P:(m + 1) * P],
                                      z_hi[:, c, :], z_lo[:, c, :])], first=False, last=(c == 2))
                    mm.then_inc(s_h1, 1)
                for c in range(4):
                    pe.wait_ge(d_h1l, 4 * s + c + 1)
                    for m in range(2):
                        mm = triple(pe, bank[m][:, :],
                                    [(w2_hi[:, c, m * P:(m + 1) * P], w2_lo[:, c, m * P:(m + 1) * P],
                                      h1_hi[:, c, :], h1_lo[:, c, :])], first=(c == 0), last=(c == 3))
                        if c == 3:
                            mm.then_inc(s_h2, 1)
                for m in range(2):
                    pe.wait_ge(a_h2, 2 * s + m + 1)
                    mm = pe.matmul(bank[2][0:1, :], w3[:, m:m + 1], h2[:, m, :], start=(m == 0), stop=(m == 1))
                mm.then_inc(s_yo, 1)

            with pe.Fori(0, SUPERS) as s:
                dense_turn(s)
                for n in range(STEPS + 2):
                    if 1 <= n <= STEPS:
                        mix_features(s, n - 1)
                    if n < STEPS:
                        turn_rows(s, n)
                    if n >= 2:
                        gram_y(s, n - 2, 0)
                    if n < STEPS:
                        times_gram(s, n)
                    if n == 0:
                        dense_product(s)
                    if n == 1:
                        dense_variance(s)
                    if n >= 2:
                        gram_y(s, n - 2, 1)
                    if 1 <= n <= STEPS:
                        project(s, n - 1, 0)
                        project(s, n - 1, 1)
                back(s)

        @block.scalar
        def _(act):
            def copy_turned(s, n):
                i0, i1 = CHUNKS[n % 4]
                act.wait_ge(s_tr, s * STEPS + n + 1)
                if n >= 2:
                    act.wait_ge(s_t, s * STEPS + n - 1)
                w = (i1 - i0) * P
                nc.scalar.activation(embt[:, n % 2, 0:w], ps_tr[:, 0:w], ACT.Copy).then_inc(a_tr, 1)

            def root_s(s, n):
                i0, i1 = CHUNKS[n % 4]
                w = 2 * (i1 - i0)
                act.wait_ge(d_var, s * STEPS + n + 1)
                nc.scalar.activation(std_s[:, 0:w], var_s[:, 0:w], ACT.Sqrt, bias=eps[:, 0:1],
                                     scale=1.0 / E).then_inc(a_std, 1)

            def u_high(s, n, g):
                act.wait_ge(s_u, s * STEPS + n + 1)
                nc.scalar.activation(upair[0:DS, n % 2, g, :], ps_u[DS * g:DS * g + DS, :], ACT.Copy).then_inc(a_hi, 1)

            def square_y(s, n, g):
                act.wait_ge(s_y, s * 2 * STEPS + 2 * n + g + 1)
                if n >= 1:
                    act.wait_ge(d_vy, s * 2 * STEPS + 2 * n + g - 1)
                nc.scalar.activation(ysq[:, g, :], ps_y[g][:, :], ACT.Square).then_inc(a_sq, 1)

            def root_y(s, n, g):
                act.wait_ge(d_vy, s * 2 * STEPS + 2 * n + g + 1)
                nc.scalar.activation(std_y[:, g, :], var_y[:, g, :], ACT.Sqrt, bias=eps[:, 0:1],
                                     scale=1.0 / PJ).then_inc(a_sdy, 1)

            def copy_gram(s, n, g):
                it, k = divmod(n, 4)
                t0 = 32 * it + 16 * g + 4 * k
                act.wait_ge(s_z, s * 2 * STEPS + 2 * n + g + 1)
                for j in range(4):
                    r = slice(32 * j, 32 * j + 32)
                    src = bank_z[r, :, 0:2 * TW].rearrange("p b (t q) -> p b t q", t=2)[:, :, :, PJ * j:PJ * (j + 1)]
                    dst = gram[r, :, t0:t0 + 4].rearrange("p q (b t) -> p b t q", b=2)
                    nc.scalar.activation(dst, src, ACT.Copy)
                src = bank_z[:, :, 0:2 * TW].rearrange("p b (t q) -> p b t q", t=2)[:, :, :, 4 * PJ:TW]
                dst = gram_x[:, :, t0:t0 + 4].rearrange("p q (b t) -> p b t q", b=2)
                nc.scalar.activation(dst, src, ACT.Copy).then_inc(a_z, 1)

            act.sem_inc(a_yo, 1)
            act.sem_inc(s_yfree, 1)
            with act.Fori(0, SUPERS) as s:
                for n in range(STEPS + 2):
                    if n == 0:
                        for c in range(2):
                            act.wait_ge(s_dt, s + 1)
                            if c == 0:
                                act.wait_ge(dp, 2)
                            nc.scalar.activation(d_hi[:, c, :], bank[5 + c][:, :], ACT.Copy).then_inc(a_dh, 1)
                    if 1 <= n <= STEPS:
                        u_high(s, n - 1, 0)
                        u_high(s, n - 1, 1)
                    if n < STEPS:
                        copy_turned(s, n)
                    if n == 1:
                        act.wait_ge(s_xp, s + 1)
                        nc.scalar.activation(xa[:], ps_x[:, :], ACT.Square).then_inc(a_xs, 1)
                    if n >= 2:
                        copy_gram(s, n - 2, 0)
                    if n < STEPS:
                        root_s(s, n)
                    if n >= 2:
                        copy_gram(s, n - 2, 1)
                    if n == 1:
                        act.wait_ge(s_xv, s + 1)
                        nc.scalar.activation(xb[:], bank[5][:, :], ACT.Sqrt, bias=eps[:, 0:1],
                                             scale=1.0 / E).then_inc(a_xd, 1)
                    if 1 <= n <= STEPS:
                        square_y(s, n - 1, 0)
                        square_y(s, n - 1, 1)
                        root_y(s, n - 1, 0)
                        root_y(s, n - 1, 1)
                for q in range(0, NG + 2, 2):
                    act.wait_ge(s_q, (NG + 2) * s + q + 1)
                    src = bank[[0, 1, 2, 7][q % 4]]
                    if q < NG:
                        w = 4 * q + 3
                        dst = feat[:, :, OFF[q]:OFF[q] + 4 * w].rearrange("t j (m p) -> t m j p", m=4)
                        last = nc.scalar.activation(dst, src[:, :].rearrange("t (m j p) -> t m j p", m=4, j=4)[:, :, :, 0:w],
                                                    ACT.Copy)
                    else:
                        for j in range(2):
                            last = nc.scalar.activation(feat[:, j, XOFF:XOFF + 2 * PJ].rearrange("t (c p) -> t c p", c=2),
                                                        own_block(src, j), ACT.Copy)
                    last.then_inc(a_f, 1)
                for c in range(FCH):
                    act.wait_ge(s_ft, FCH * s + c + 1)
                    nc.scalar.activation(f_hi[:, c, :], bank[[0, 1, 2, 7, 3][c]][:, :], ACT.Copy).then_inc(a_fh, 1)
                for j in range(4):
                    act.wait_ge(d_ag, 4 * s + j + 1)
                    nc.scalar.activation(std_o[:, j:j + 1], mv[:, j, 1:2], ACT.Sqrt, bias=eps[:, 0:1]).then_inc(a_sdo, 1)
                    act.wait_ge(d_sh, 4 * s + j + 1)
                    nc.scalar.activation(zn[:, j, :], bank[[4, 5, 6, 0][j]][:, 0:KUSE], ACT.Identity,
                                         bias=shift_o[:, j:j + 1], scale=rstd_o[:, j:j + 1]).then_inc(a_zn, 1)
                act.wait_ge(s_zt, s + 1)
                for c in range(3):
                    nc.scalar.activation(z_hi[:, c, :], bank[[1, 2, 7][c]][:, :], ACT.Copy).then_inc(a_zh, 1)
                for m in range(4):
                    act.wait_ge(s_h1, 4 * s + m + 1)
                    nc.scalar.activation(h1f[m], bank[3 + m][:, :], ACT.Relu, bias=b1z[:, m:m + 1]).then_inc(a_h1, 1)
                for m in range(2):
                    act.wait_ge(s_h2, 2 * s + m + 1)
                    nc.scalar.activation(h2[:, m, :], bank[m][:, :], ACT.Relu, bias=b2[:, m:m + 1]).then_inc(a_h2, 1)
                act.wait_ge(s_yo, s + 1)
                act.wait_ge(s_yfree, s + 1)
                nc.scalar.activation(yrow[0:1, :].rearrange("o (t j) -> o t j", j=4),
                                     bank[2][0:1, :].rearrange("o (j t) -> o t j", j=4), ACT.Copy).then_inc(a_yo, 1)

        @block.vector
        def _(dve):
            V = nc.vector
            chain = [0]
            s_chain = s_prep_chain

            def link(ins):
                chain[0] += 1
                ins.then_inc(s_chain, 1)
                dve.wait_ge(s_chain, chain[0])

            dve.sem_inc(d_sc, 8)
            V.memset(ones[:], 1.0).then_inc(s_chain, 1)
            V.memset(eps[:], EPS).then_inc(s_chain, 1)
            V.memset(bs_st[:].bitcast(F32), 0.0).then_inc(s_chain, 1)
            V.memset(bs_mv[:].bitcast(F32), 0.0).then_inc(s_chain, 1)
            V.memset(tvec[:], 1.0).then_inc(s_chain, 1)
            chain[0] = 5
            dve.wait_ge(s_const, 16 * NLOAD)
            link(V.memset(bmat, 0.0))
            lo = ROFF - 4 * P
            for c in range(FCH):
                link(V.tensor_scalar(bmat[:, c, lo:lo + QC], ind_p[:, c, :], bb[:, c:c + 1], None, ALU.mult))
                link(V.scalar_tensor_tensor(bmat[:, c, lo:lo + QC], ind_q[:, c, :], ba[:, c:c + 1],
                                            bmat[:, c, lo:lo + QC], ALU.mult, ALU.add))
                link(V.tensor_scalar(bmat[:, c, lo + QC - 1:lo + QC], ba[:, c:c + 1], bb[:, c:c + 1], float(E),
                                     ALU.mult, ALU.mult))
            dve.wait_ge(pp, 1)
            for g in range(2):
                link(V.tensor_copy(wsc2[:, g, :], bank[0][:, 0:DS]))
            link(V.tensor_scalar(wg2[:], wsc2[:], gs[:, 0:1], None, ALU.mult))
            link(V.tensor_copy(wsit[:], bank[2][0:NF, 0:PJ]))
            link(V.tensor_copy(wd_hi[:].rearrange("p c e -> p (c e)"), bank[1][:, 0:DD]))
            V.tensor_tensor(wd_lo[:].rearrange("p c e -> p (c e)"), bank[1][:, 0:DD],
                            wd_hi[:].rearrange("p c e -> p (c e)").bitcast(F32), ALU.subtract).then_inc(dp, 1)
            dve.wait_ge(pp, 2)
            link(V.tensor_tensor(gram2[:], bank[3][:, 0:P], blockmask[:], ALU.mult))
            link(V.tensor_copy(wg_hi[:], bank[4][:, 0:P]))
            link(V.tensor_tensor(wg_lo[:], bank[4][:, 0:P], wg_hi[:].bitcast(F32), ALU.subtract))
            for w in range(WINDOW):
                link(V.tensor_tensor(mix[:, :, w, :], bank[5][:, 0:TILES * PJ].rearrange("p (i q) -> p i q", q=PJ),
                                     window[:, :, w:w + 1].to_broadcast([P, TILES, PJ]), ALU.mult))
            rowsum = [bank[6][32 * k:32 * k + 1, 0:PJ].unsqueeze(1).to_broadcast([1, BS, PJ]) for k in range(4)]
            for k in range(4):
                r = slice(32 * k, 32 * k + 1)
                link(V.tensor_copy(bs_mv[r], rowsum[k]))
                if k % 2:
                    link(V.tensor_tensor(bs_mv[r], rowsum[k], bs_mv[r].bitcast(F32), ALU.subtract))
                link(V.tensor_copy(bs_st[r], bs4[r, :]))
                if k >= 2:
                    link(V.tensor_tensor(bs_st[r], bs4[r, :], bs_st[r].bitcast(F32), ALU.subtract))
            for c in range(FCH):
                link(V.tensor_scalar(wl_raw[:, c, :], wl_raw[:, c, :], ga[:, c:c + 1], gb[:, c:c + 1], ALU.mult, ALU.mult))
                if c == FCH - 1:
                    link(V.scalar_tensor_tensor(wl_raw[:, c, :], bank[7][:, :], gr[:, 0:1], wl_raw[:, c, :],
                                                ALU.mult, ALU.add))
            link(V.tensor_copy(wl_hi[:], wl_raw))
            link(V.tensor_tensor(wl_lo[:], wl_raw, wl_hi[:].bitcast(F32), ALU.subtract))
            link(V.tensor_tensor(b1z[:], bank[0][:, 256:260], b1[:], ALU.add))
            for c in range(3):
                link(V.tensor_scalar(w1_raw[:, c, :], w1_raw[:, c, :], gl[:, c:c + 1], None, ALU.mult))
            link(V.tensor_copy(w1_hi[:], w1_raw))
            link(V.tensor_tensor(w1_lo[:], w1_raw, w1_hi[:].bitcast(F32), ALU.subtract))
            link(V.tensor_copy(w2_hi[:], w2_raw))
            link(V.tensor_tensor(w2_lo[:], w2_raw, w2_hi[:].bitcast(F32), ALU.subtract))
            link(V.memset(feat[:, :, ONEOFF:FEAT], 0.0))
            V.memset(feat[:, :, ONEOFF:ONEOFF + 1], 1.0).then_inc(dp, 1)

            def u_low(s, n, g):
                dve.wait_ge(a_hi, s * 2 * STEPS + 2 * n + g + 1)
                V.tensor_tensor(upair[DS:P, n % 2, g, :], ps_u[DS * g:DS * g + DS, :],
                                upair[0:DS, n % 2, g, :].bitcast(F32), ALU.subtract).then_inc(d_lo_u, 1)

            def variance_s(s, n):
                it, c = divmod(n, 4)
                i0, i1 = CHUNKS[c]
                w = 2 * (i1 - i0)
                dve.wait_ge(s_t, s * STEPS + n + 1)
                V.tensor_tensor(prod[:, 0:w, :], ps_t[:, 0:w * DS].rearrange("p (w d) -> p w d", d=DS),
                                emb[it % 2][:, i0:i1, :, :].rearrange("p i g d -> p (i g) d"),
                                ALU.mult).then_inc(d_prod, 1)
                dve.wait_ge(d_prod, s * STEPS + n + 1)
                V.tensor_reduce(var_s[:, 0:w], prod[:, 0:w, :], AX.X, ALU.add).then_inc(d_var, 1)

            def scale_s(s, n):
                it, c = divmod(n, 4)
                i0, i1 = CHUNKS[c]
                w = 2 * (i1 - i0)
                dve.wait_ge(a_std, s * STEPS + n + 1)
                V.reciprocal(rstd_s[:, 0:w], std_s[:, 0:w]).then_inc(d_rs, 1)
                dve.wait_ge(d_rs, s * STEPS + n + 1)
                V.tensor_tensor(scaled[:, i0:i1, :, :].rearrange("p i g d -> p (i g) d"),
                                emb[it % 2][:, i0:i1, :, :].rearrange("p i g d -> p (i g) d"),
                                rstd_s[:, 0:w].unsqueeze(2).to_broadcast([P, w, DS]), ALU.mult).then_inc(d_sc, 1)

            def variance_y(s, n, g):
                dve.wait_ge(a_sq, s * 2 * STEPS + 2 * n + g + 1)
                V.tensor_reduce(var_y[:, g, :], ysq[:, g, :].rearrange("p (s q) -> p s q", q=PJ), AX.X,
                                ALU.add).then_inc(d_vy, 1)

            def norm_y(s, n, g):
                dve.wait_ge(a_sdy, s * 2 * STEPS + 2 * n + g + 1)
                V.reciprocal(rstd_y[:, g, :], std_y[:, g, :]).then_inc(d_ry, 1)
                dve.wait_ge(d_ry, s * 2 * STEPS + 2 * n + g + 1)
                V.tensor_tensor(tvec[:, n % 2, g, :, 0:4 * PJ].rearrange("p t (j q) -> p t j q", j=4),
                                ps_y[g][:, :].rearrange("p (t j q) -> p t j q", t=4, j=4),
                                rstd_y[:, g, :].rearrange("p (t j) -> p t j", t=4).unsqueeze(3).to_broadcast(
                                    [P, 4, 4, PJ]), ALU.mult).then_inc(d_t, 1)

            def x_column(s, n):
                it, k = divmod(n, 4)
                if n == 0:
                    dve.wait_ge(d_xt, s + 1)
                if n >= 2:
                    dve.wait_ge(s_z, s * 2 * STEPS + 2 * n - 2)
                for g in range(2):
                    t0 = 32 * it + 16 * g + 4 * k
                    last = V.tensor_copy(tvec[:, n % 2, g, :, 4 * PJ:TW:2],
                                         xt[:, :, t0:t0 + 4].rearrange("p j t -> p t j"))
                last.then_inc(d_x, 1)

            with dve.Fori(0, SUPERS) as s:
                for n in range(STEPS + 1):
                    if n == 0:
                        for c in range(2):
                            dve.wait_ge(a_dh, 2 * s + c + 1)
                            V.tensor_tensor(d_lo[:, c, :], bank[5 + c][:, :], d_hi[:, c, :].bitcast(F32),
                                            ALU.subtract).then_inc(d_dl, 1)
                    if n >= 1:
                        u_low(s, n - 1, 0)
                        u_low(s, n - 1, 1)
                    if n < STEPS:
                        variance_s(s, n)
                        scale_s(s, n)
                    if n == 1:
                        dve.wait_ge(a_xd, s + 1)
                        V.reciprocal(xb[:], xb[:]).then_inc(d_xr, 1)
                        dve.wait_ge(d_xr, s + 1)
                        V.tensor_tensor(xb[:], ps_x[:, :], xb[:], ALU.mult).then_inc(d_xn, 1)
                        dve.wait_ge(d_xn, s + 1)
                        V.tensor_scalar(xt[:].rearrange("p j t -> p (j t)"), xb[:], gd[:, 0:1], bd[:, 0:1],
                                        ALU.mult, ALU.add).then_inc(d_xt, 1)
                    if n >= 1:
                        x_column(s, n - 1)
                        variance_y(s, n - 1, 0)
                        variance_y(s, n - 1, 1)
                        norm_y(s, n - 1, 0)
                        norm_y(s, n - 1, 1)
                for q in range(1, NG + 2, 2):
                    dve.wait_ge(s_q, (NG + 2) * s + q + 1)
                    if q > NG:
                        for j in range(2, 4):
                            last = V.tensor_copy(feat[:, j, XOFF:XOFF + 2 * PJ].rearrange("t (c p) -> t c p", c=2),
                                                 own_block(bank[1], j))
                        last.then_inc(d_f, 1)
                        continue
                    w = 4 * q + 3
                    V.tensor_copy(feat[:, :, OFF[q]:OFF[q] + 4 * w].rearrange("t j (m p) -> t m j p", m=4),
                                  bank[[0, 1, 2, 7][q % 4]][:, :].rearrange("t (m j p) -> t m j p", m=4, j=4)[:, :, :, 0:w]
                                  ).then_inc(d_f, 1)
                dve.wait_ge(s_sx, s + 1)
                V.tensor_copy(feat[:, :, SXOFF:SXOFF + 1].rearrange("t j o -> t (j o)"), bank[3][:, 0:4]).then_inc(d_f, 1)
                for c in range(FCH):
                    dve.wait_ge(a_fh, FCH * s + c + 1)
                    V.tensor_tensor(f_lo[:, c, :], bank[[0, 1, 2, 7, 3][c]][:, :], f_hi[:, c, :].bitcast(F32),
                                    ALU.subtract).then_inc(d_fl, 1)
                for j in range(4):
                    dve.wait_ge(s_o, 4 * s + j + 1)
                    V.bn_stats(stats[:, j, :], bank[[4, 5, 6, 0][j]][:, :]).then_inc(d_bn, 1)
                    dve.wait_ge(d_bn, 4 * s + j + 1)
                    dve.sem_inc(s_seen, 1)
                    V.bn_aggr(mv[:, j, :], stats[:, j, :]).then_inc(d_ag, 1)
                    dve.wait_ge(a_sdo, 4 * s + j + 1)
                    V.reciprocal(rstd_o[:, j:j + 1], std_o[:, j:j + 1]).then_inc(d_ro, 1)
                    dve.wait_ge(d_ro, 4 * s + j + 1)
                    V.tensor_scalar(shift_o[:, j:j + 1], mv[:, j, 0:1], rstd_o[:, j:j + 1], -1.0, ALU.mult,
                                    ALU.mult).then_inc(d_sh, 1)
                for c in range(3):
                    dve.wait_ge(a_zh, 3 * s + c + 1)
                    V.tensor_tensor(z_lo[:, c, :], bank[[1, 2, 7][c]][:, :], z_hi[:, c, :].bitcast(F32),
                                    ALU.subtract).then_inc(d_zl, 1)
                for m in range(4):
                    dve.wait_ge(a_h1, 4 * s + m + 1)
                    V.tensor_copy(h1_hi[:, m, :], h1f[m]).then_inc(d_h1h, 1)
                    dve.wait_ge(d_h1h, 4 * s + m + 1)
                    V.tensor_tensor(h1_lo[:, m, :], h1f[m], h1_hi[:, m, :].bitcast(F32), ALU.subtract).then_inc(d_h1l, 1)


def constants():
    r = np.arange(P)
    c = {"c_ident": np.eye(P), "c_center": np.eye(P) - 1.0 / E,
         "c_blockmask": np.kron(np.eye(2), np.ones((DS, DS))), "c_center_p": np.eye(PJ) - 1.0 / PJ}
    row = P * np.arange(TILES)[None, :] + r[:, None]
    c["c_spread"] = (np.arange(NF)[:, None, None] == (row % NF).T[None])
    first = np.array([first_sample(i) for i in range(TILES)])
    c["c_window"] = (row // NF - first)[:, :, None] == np.arange(WINDOW)
    p, q, col = feature_map()
    ip, iq = np.zeros((FEAT, QC)), np.zeros((FEAT, QC))
    for f in range(FEAT):
        if q[f] >= 0:
            ip[f, p[f]] = 1
            iq[f, q[f]] = 1
        elif p[f] >= 0:
            iq[f, PJ] = 1
    c["c_ind_p"] = ip.reshape(FCH, P, QC).transpose(1, 0, 2)
    c["c_ind_q"] = iq.reshape(FCH, P, QC).transpose(1, 0, 2)
    return {k: np.ascontiguousarray(v, dtype=np.float32) for k, v in c.items()}


def feature_map():
    p, q, col = (np.full(FEAT, -1) for _ in range(3))
    for g in range(NG):
        w = 4 * g + 3
        for m in range(4):
            for x in range(w):
                y = 4 * g + m
                if x < y:
                    f = OFF[g] + m * w + x
                    p[f], q[f], col[f] = x, y, (y + 1) * y // 2 + x + 1
    for x in range(PJ):
        p[XOFF + x], col[XOFF + x] = x, (x + 1) * x // 2
    return p, q, col


def kernel(**inputs):
    import concourse.bacc as _bacc
    from concourse.bass_utils import run_bass_kernel_spmd as _run

    x = {k: np.asarray(v) for k, v in inputs.items()}
    table = np.concatenate([x[f"tbl_{f}"] for f in range(NF)], axis=0)
    begin = np.cumsum([0] + [x[f"tbl_{f}"].shape[0] for f in range(NF - 1)])
    row = P * np.arange(TILES)[None, :] + np.arange(P)[:, None]
    p, q, col = feature_map()

    def place(v, where, none):
        full = np.full((FEAT,) + v.shape[1:], none, np.float32)
        full[where >= 0] = v[where[where >= 0]]
        return np.ascontiguousarray(full.reshape((FCH, P) + v.shape[1:]).swapaxes(0, 1))

    def cols(v, n):
        return np.ascontiguousarray(v.reshape(n, P).T)

    gsi, bsi = x["L0_rec_gsi"], x["L0_rec_bsi"]
    gr = np.zeros((P, 1), np.float32)
    gr[ROFF - 4 * P:ROFF - 4 * P + PJ, 0] = gsi
    gr[SXOFF - 4 * P:ONEOFF - 4 * P + 1, 0] = 1.0
    w1 = x["W_top1"].reshape(6, P, H1)
    arrays = {
        "table": table,
        "ids": np.ascontiguousarray(x["ids"].reshape(-1, P).T).reshape(P, ITERS * SUPERS, 2, TILES),
        "c_base": np.ascontiguousarray(begin[row % NF].astype(np.int32)),
        "dense": np.ascontiguousarray(x["r_dense_t"]).reshape(SUPERS * P, 4, DD),
        "Ws": x["L0_rec_Ws"], "Wd": x["L0_rec_Wd"], "Wsi": x["L0_rec_Wsi"],
        "gs": x["L0_rec_gs"].reshape(P, 1), "bs": x["L0_rec_bs"].reshape(1, P),
        "gd": x["L0_rec_gd"].reshape(P, 1), "bd": x["L0_rec_bd"].reshape(P, 1),
        "Wl": place(x["L0_rec_Wl"].T, col, 0.0),
        "ga": place(gsi, p, 1.0), "gb": place(gsi, q, 1.0), "ba": place(bsi, p, 0.0), "bb": place(bsi, q, 0.0),
        "gr": gr, "gl": cols(x["L0_rec_gl"][:KUSE], 3), "bl": cols(x["L0_rec_bl"][:KUSE], 3),
        "W1": np.ascontiguousarray(w1[[0, 1, 2, 4, 5]].transpose(1, 0, 2)), "b1": cols(x["b_top1"], 4),
        "W2": np.ascontiguousarray(x["W_top2"].reshape(4, P, H2).transpose(1, 0, 2)), "b2": cols(x["b_top2"], 2),
        "w3": cols(x["W_top3"], 2),
        **constants(),
    }
    nc = _bacc.Bacc("TRN2", target_bir_lowering=False, num_devices=1)
    a, feed = {}, {}
    for name, v in arrays.items():
        v = np.ascontiguousarray(v)
        feed[f"in_{name}"] = v
        a[name] = nc.dram_tensor(f"in_{name}", v.shape, mybir.dt.from_np(v.dtype), kind="ExternalInput").ap()
    out = nc.dram_tensor("out_y", (SUPERS, SUPER), F32, kind="ExternalOutput").ap()
    build(nc, a, out)
    r = _run(nc, [feed], core_ids=[0])
    return r.results[0]["out_y"].reshape(BATCH, 1)
```

```python
from contextlib import ExitStack

import numpy as np
import concourse.bass as bass
from concourse import mybir

F32 = mybir.dt.float32
F32R = mybir.dt.float32r
I32 = mybir.dt.int32
ALU = mybir.AluOpType
ACT = mybir.ActivationFunctionType
AX = mybir.AxisListType

P = 128
NF = 26
DS = 64
E = 128
PJ = 32
DD = 256
KOUT = 512
KUSE = 384
H1, H2 = 512, 256
EPS = 1e-5
BATCH = 2048
SUPERS = 4
ITERS = 4
SUPER = BATCH // SUPERS
GROUP = 64
TILES = GROUP * NF // P
CHUNKS = [(0, 4), (4, 7), (7, 10), (10, 13)]
STEPS = ITERS * len(CHUNKS)
BS = GROUP // 4
QC = PJ + 2
TW = 4 * PJ + 8
NG = PJ // 4
OFF = [sum(4 * (4 * h + 3) for h in range(g)) for g in range(NG + 1)]
XOFF, ROFF, SXOFF, ONEOFF = OFF[NG], OFF[NG] + PJ, OFF[NG] + 2 * PJ, OFF[NG] + 2 * PJ + 1
FCH = 5
FEAT = FCH * P
WINDOW = 6
BM = ONEOFF - 4 * P + 1
VECS, VN = {}, 0
for _name, _n in (("gs", 1), ("gd", 1), ("bd", 1), ("gr", 1), ("ga", FCH), ("gb", FCH), ("ba", FCH), ("bb", FCH),
                  ("gl", 3), ("bl", 3), ("b1", 4), ("b2", 2), ("w3", 2), ("rowmask", 4)):
    VECS[_name] = (VN, _n)
    VN += _n


def first_sample(i):
    return P * i // NF


def last_sample(i):
    return (P * i + P - 1) // NF


def u_pieces(k):
    out = []
    for i in range(TILES):
        a, b = max(first_sample(i), BS * k), min(last_sample(i) + 1, BS * (k + 1))
        if a < b:
            out.append((i, a, b))
    return out


def parts(name, last, each, slots):
    total, out, at = last * each, [], 0
    for i in range(len(slots)):
        end = total * (i + 1) // len(slots)
        items = []
        while at < end:
            k = at // each
            stop = min(end, (k + 1) * each)
            items.append((name, k, at - k * each, stop - k * each))
            at = stop
        out.append((slots[i], items))
    return out


SLOTS = [[] for _ in range(2 * STEPS)]
for _at, _items in ([(0, [("dense_turn", 0), ("dense_turn", 1)]), (1, [("dense_product", 0)]),
                     (2, [("x_sums", 0)]), (3, [("x_spread", 0)]),
                     (4, [("turn_gram", 0), ("turn_gram", 1)]), (5, [("turn_gram", 2), ("turn_gram", 3)]),
                     (6, [("turn_gram", 4), ("turn_gram", 5)]), (7, [("turn_gram", 6)]),
                     (8, [("turn_gram", 7), ("turn_gram", 8)]), (9, [("turn_gram", 9)]),
                     (10, [("move_early", 0), ("turn_feat", 0), ("turn_feat", 1)]),
                     (11, [("turn_feat", 2), ("turn_feat", 3)]), (12, [("turn_feat", 4)])]
                    + parts("linear", 4, 15, range(13, 19))
                    + [(19, [("turn_dense", 0), ("turn_dense", 1)]), (20, [("turn_z", 0), ("turn_z", 1)]),
                       (21, [("turn_z", 2)])]
                    + parts("layer1", 4, 15, range(22, 28)) + parts("layer2", 2, 12, range(28, 31))
                    + [(31, [("layer3", 0), ("sum_x", 0)])]):
    SLOTS[_at] += _items
OF_THIS_SUPER = ("sum_x", "dense_turn", "dense_product", "x_sums", "x_spread", "move_early")
EARLY = 3
PRODUCTS = {"linear": 15, "layer1": 15, "layer2": 12}


def run_slot(stage, at, s, b, whole):
    for name, k, *cut in SLOTS[at]:
        if name == "sum_x" and b is None:
            continue
        of = s if name in OF_THIS_SUPER else b
        if of is None or name not in stage:
            continue
        if not cut:
            stage[name](of, k)
        elif not whole:
            stage[name](of, k, *cut)
        elif cut[1] == PRODUCTS[name]:
            stage[name](of, k)


def after(s, n, k=1):
    return not isinstance(s, int) or STEPS * s + n >= k


def back_to(s, n):
    if n >= 0:
        return (s, n) if not isinstance(s, int) or s < SUPERS else None
    if isinstance(s, int) and s == 0:
        return None
    return (s - 1, n + STEPS)


def build(nc, a, out):
    ctx = ExitStack()
    with ctx:
        def sb(name, shape, dt=F32):
            return ctx.enter_context(nc.sbuf_tensor(name, shape, dt))

        def psum(name, shape):
            return ctx.enter_context(nc.psum_tensor(name, shape, F32))

        def sem(name):
            return ctx.enter_context(nc.semaphore(name))

        ps_t = psum("ps_t", [P, 512])
        ps_u = psum("ps_u", [P, 512])
        ps_y = [psum(f"ps_y{g}", [P, 512]) for g in range(2)]
        ps_z = psum("ps_z", [P, 2, 512])
        ps_b = [psum(f"ps_b{i}", [P, 512]) for i in range(2)]

        big = sb("big", [P, 3 * P + TILES * WINDOW])
        ident, center, blockmask = big[:, 0:P], big[:, P:2 * P], big[:, 2 * P:3 * P]
        window = big[:, 3 * P:].rearrange("p (i w) -> p i w", w=WINDOW)
        small = sb("small", [PJ, PJ + NF])
        center_p, wsi = small[:, 0:PJ], small[:, PJ:PJ + NF]
        inds = sb("inds", [P, 2, FCH, QC])
        ind_p, ind_q = inds[:, 0], inds[:, 1]
        vecs = sb("vecs", [P, VN])

        def vec(name):
            at, n = VECS[name]
            return vecs[:, at:at + n]

        gs, gd, bd, gr = vec("gs"), vec("gd"), vec("bd"), vec("gr")
        ga, gb, ba, bb = vec("ga"), vec("gb"), vec("ba"), vec("bb")
        gl, bl, b1, b2, w3, rowmask = vec("gl"), vec("bl"), vec("b1"), vec("b2"), vec("w3"), vec("rowmask")
        ones = sb("ones", [P, P])
        eps = sb("eps", [P, 1])
        wsd = sb("wsd", [P, DS + DD])
        ws, wd = wsd[:, 0:DS], wsd[:, DS:DS + DD]
        bsr = sb("bsr", [P, E])
        wsc2 = sb("wsc2", [P, 2, DS])
        wg2 = sb("wg2", [P, 2, DS])
        gram2 = sb("gram2", [P, P])
        wg_hi, wg_lo = sb("wg_hi", [P, E], F32R), sb("wg_lo", [P, E], F32R)
        wsit = sb("wsit", [NF, PJ])
        mix = sb("mix", [P, TILES, WINDOW, PJ])
        wd_hi, wd_lo = sb("wd_hi", [P, 2, E], F32R), sb("wd_lo", [P, 2, E], F32R)
        wl_hi, wl_lo = sb("wl_hi", [P, FCH, KOUT], F32R), sb("wl_lo", [P, FCH, KOUT], F32R)
        w1_hi, w1_lo = sb("w1_hi", [P, 5, H1], F32R), sb("w1_lo", [P, 5, H1], F32R)
        w2_hi, w2_lo = sb("w2_hi", [P, 4, H2], F32R), sb("w2_lo", [P, 4, H2], F32R)
        b1z = sb("b1z", [P, 4])

        ids = sb("ids", [P, ITERS * SUPERS, 2, TILES], I32)
        base = sb("base", [P, TILES], I32)
        rows_now = [sb(f"rows_now{i}", [P, 2, TILES], I32) for i in range(ITERS)]
        emb = [sb(f"emb{i}", [P, TILES, 2, DS]) for i in range(2)]
        scaled = sb("scaled", [P, TILES, 2, DS])
        embt = sb("embt", [P, 4 * P])
        prod = sb("prod", [P, 8, DS])
        var_s, std_s, rstd_s = sb("var_s", [P, 8]), sb("std_s", [P, 8]), sb("rstd_s", [P, 8])
        upair = sb("upair", [P, 2, 512], F32R)
        ushift = sb("ushift", [P, 2, 512], F32R)
        ysq = sb("ysq", [P, 2, 512])
        var_y, std_y, rstd_y = sb("var_y", [P, 2, BS]), sb("std_y", [P, 2, BS]), sb("rstd_y", [P, 2, BS])
        tvec = sb("tvec", [P, 2, 2, 4, TW])
        gram_all, gram_early = sb("gram_all", [P, PJ + 8, P]), sb("gram_early", [P, PJ + 8, 2, 4 * EARLY])

        dense = sb("dense", [P, 4, DD])
        d_hi, d_lo = sb("d_hi", [P, 2, 512], F32R), sb("d_lo", [P, 2, 512], F32R)
        xa, xb = sb("xa", [P, 512]), sb("xb", [P, 512])
        std_x, rstd_x = sb("std_x", [P, 4]), sb("rstd_x", [P, 4])
        xt = sb("xt", [P, 4, P])
        feat = sb("feat", [P, 4, FEAT])
        f_hi, f_lo = sb("f_hi", [P, FCH, 512], F32R), sb("f_lo", [P, FCH, 512], F32R)
        stats, mv = sb("stats", [P, 4, 6]), sb("mv", [P, 4, 2])
        std_o, rstd_o = sb("std_o", [P, 4]), sb("rstd_o", [P, 4])
        zn = sb("zn", [P, 4, KUSE])
        z_hi, z_lo = sb("z_hi", [P, 3, 512], F32R), sb("z_lo", [P, 3, 512], F32R)
        yrow = sb("yrow", [1, 512])
        shift_t = prod[:].rearrange("p w d -> p (w d)").rearrange("p (k e) -> p k e", k=4)
        w_raw = feat[:].rearrange("p j f -> p (j f)").rearrange("p (c m) -> p c m", c=5)
        zn_flat = zn[:].rearrange("p j k -> p (j k)")
        w2_raw = zn_flat[:, 0:4 * H2].rearrange("p (c m) -> p c m", c=4)
        bmat = zn_flat[:, 4 * H2:4 * H2 + FCH * BM].rearrange("p (c m) -> p c m", c=FCH)
        spread = scaled[0:NF].rearrange("p i g d -> p i (g d)")
        h1_hi, h1_lo = f_hi[:, 0:4, :], f_lo[:, 0:4, :]
        h2 = zn_flat[:, 0:2 * 512].rearrange("p (m b) -> p m b", m=2)
        h1f = [feat[:, m, 0:512] for m in range(4)]

        s_ids, s_dense, s_out = sem("ids_loaded"), sem("dense_loaded"), sem("out_stored")
        s_const, s_vecs, s_wl, s_w1, s_w2 = (sem("front_weights_loaded"), sem("vectors_loaded"), sem("wl_loaded"),
                                             sem("w1_loaded"), sem("w2_loaded"))
        s_idx, s_now = sem("row_numbers_ready"), sem("rows_now_ready")
        s_seen = sem("wait_carrier")
        s_row = [[sem(f"rows_landed_{b}_{i}") for i in range(TILES)] for b in range(2)]
        pp, dp, pw, dw, s_chain = (sem("prep_pe"), sem("prep_dve"), sem("back_weights_pe"), sem("back_weights_dve"),
                                   sem("prep_chain"))
        s_tr, s_t, s_u, s_y, s_z = sem("embt_done"), sem("t_done"), sem("u_done"), sem("y_done"), sem("gram_done")
        s_dt, s_xp, s_xv, s_xs = sem("dense_turned"), sem("x_product"), sem("x_variance"), sem("rstd_x_spread")
        s_q, s_sx, s_ft, s_o = sem("gram_turned"), sem("sum_x_done"), sem("feat_turned"), sem("block_out")
        s_zt, s_et, s_h1, s_h2, s_yo = (sem("z_turned"), sem("dense_turned_again"), sem("h1_product"),
                                        sem("h2_product"), sem("y_product"))
        s_yfree = sem("y_row_free")
        a_tr, a_std, a_hi, a_sq, a_sdy, a_z = (sem("embt_copied"), sem("std_s_ready"), sem("u_high"), sem("y_squared"),
                                               sem("std_y_ready"), sem("gram_copied"))
        a_dh, a_xs, a_xd = sem("dense_high"), sem("x_squared"), sem("std_x_ready")
        a_f, a_fh, a_sdo, a_zn, a_zh, a_eh = (sem("feat_by_act"), sem("feat_high"), sem("std_o_ready"), sem("z_ready"),
                                              sem("z_high"), sem("dense_high_again"))
        a_h1, a_h2, a_yo = sem("h1_ready"), sem("h2_ready"), sem("y_row_ready")
        d_prod, d_var, d_rs, d_sc, d_lo_u = (sem("t_times_s"), sem("var_s_ready"), sem("rstd_s_ready"),
                                             sem("rows_scaled"), sem("u_low"))
        d_vy, d_ry, d_t, d_x = sem("var_y_ready"), sem("rstd_y_ready"), sem("tvec_ready"), sem("x_in_tvec")
        d_dl, d_xr, d_xr2, d_dg, d_xn, d_xt = (sem("dense_low"), sem("rstd_x_ready"), sem("rstd_x_copied"), sem("rstd_x_on_diagonal"),
                                        sem("x_normed"), sem("xt_ready"))
        d_early = sem("early_moved")
        d_f, d_fl, d_bn, d_ag, d_ro, d_zl, d_el = (sem("feat_by_dve"), sem("feat_low"), sem("stats_ready"),
                                                   sem("mean_var_ready"), sem("rstd_o_ready"), sem("z_low"),
                                                   sem("dense_low_again"))
        d_h1h, d_h1l = sem("h1_high"), sem("h1_low")

        block = ctx.enter_context(nc.Block())

        def own_block(b, j):
            return b[:, 256 * (j % 2):256 * (j % 2 + 1)].rearrange("t (c j p) -> t c j p", c=2, j=4)[:, :, j, :]

        def gram_place(n, g):
            it, k = divmod(n, 4)
            return 32 * it + 16 * g + 4 * k

        @block.sync
        def _(sp):
            sp.dma_start(ids[:], a["ids"]).then_inc(s_ids, 16)
            sp.dma_start(base[:], a["c_base"]).then_inc(s_ids, 16)
            sp.dma_start(big[:], a["c_big"]).then_inc(s_const, 16)
            sp.dma_start(wsd[:], a["Wsd"]).then_inc(s_const, 16)
            sp.dma_start(small[:], a["small"]).then_inc(s_const, 16)
            sp.dma_start(vecs[:], a["vecs"]).then_inc(s_const, 16)
            sp.dma_start(spread, a["c_spread"]).then_inc(s_const, 16)
            sp.dma_start(bsr[:], a["bs"].to_broadcast([P, E])).then_inc(s_const, 16)

            def load_dense(s):
                sp.dma_start(dense[:], a["dense"][bass.ds(s * P, P), :, :]).then_inc(s_dense, 16)

            def store(b):
                sp.wait_ge(a_yo, b + 2)
                sp.dma_start(out[bass.ds(b, 1), :], yrow[0:1, :]).then_inc(s_out, 16)
                sp.wait_ge(s_out, 16 * b + 16)
                sp.sem_inc(s_yfree, 1)

            load_dense(0)
            sp.dma_start(inds[:], a["c_inds"]).then_inc(s_wl, 16)
            sp.dma_start(w_raw, a["Wl"]).then_inc(s_wl, 16)
            sp.dma_start(w2_raw, a["W2"]).then_inc(s_w2, 16)
            sp.wait_ge(s_dt, 2)
            load_dense(1)
            sp.wait_ge(dw, 2)
            sp.dma_start(w_raw, a["W1"]).then_inc(s_w1, 16)
            with sp.Fori(1, SUPERS - 1) as s:
                sp.wait_ge(s_dt, 2 * s + 2)
                load_dense(s - 1)
                sp.wait_ge(s_et, 2 * s)
                load_dense(s + 1)
                store(s - 1)
            sp.wait_ge(s_dt, 2 * SUPERS)
            load_dense(SUPERS - 2)
            sp.wait_ge(s_et, 2 * SUPERS - 2)
            load_dense(SUPERS - 1)
            store(SUPERS - 2)
            store(SUPERS - 1)

        @block.gpsimd
        def _(pool):
            pool.wait_ge(s_ids, 32)
            nc.gpsimd.tensor_tensor(ids[:].rearrange("p t g i -> p (t g) i"), ids[:].rearrange("p t g i -> p (t g) i"),
                                    base[:].unsqueeze(1).to_broadcast([P, 2 * ITERS * SUPERS, TILES]),
                                    ALU.add).then_inc(s_idx, 1)
            pool.wait_ge(s_idx, 1)
            with pool.Fori(0, SUPERS) as s:
                for it in range(ITERS):
                    b = it % 2
                    nc.gpsimd.tensor_copy(rows_now[it][:], ids[:, bass.ds(ITERS * s + it, 1), :, :].rearrange(
                        "p t g i -> p (t g) i")).then_inc(s_now, 1)
                    pool.wait_ge(s_now, ITERS * s + it + 1)
                    for c, (i0, i1) in enumerate(CHUNKS):
                        pool.wait_ge(d_sc, STEPS * s + 4 * it + c + 1)
                        pool.sem_inc(s_seen, 1)
                        for i in range(i0, i1):
                            for g in range(2):
                                nc.gpsimd.indirect_dma_start(
                                    emb[b][:, i, g, :], None, a["table"],
                                    bass.IndirectOffsetOnAxis(ap=rows_now[it][:, g, i:i + 1], axis=0),
                                ).then_inc(s_row[b][i], 16)

        @block.tensor
        def _(pe):
            def triple(dst, stationary, moving, first, last):
                (sh, sl), (mh, ml) = stationary, moving
                pe.matmul(dst, sh, mh, start=first, stop=False)
                pe.matmul(dst, sh, ml, start=False, stop=False)
                return pe.matmul(dst, sl, mh, start=False, stop=last)

            pe.wait_ge(s_const, 16 * 6)
            pe.matmul(ps_t[:, 0:DS], center, ws, start=True, stop=True)
            for c in range(2):
                pe.matmul(ps_u[:, c * E:(c + 1) * E], wd[:, c * P:(c + 1) * P], center, start=True, stop=True)
            pe.matmul(ps_y[0][0:NF, 0:PJ], wsi, center_p, start=True, stop=True).then_inc(pp, 1)
            pe.wait_ge(dp, 1)
            pe.matmul(ps_t[:, 0:P], wsc2[:].rearrange("p a d -> p (a d)"), wsc2[:].rearrange("p a d -> p (a d)"),
                      start=True, stop=True)
            pe.transpose(ps_u[:, 0:P], wg2[:].rearrange("p a d -> p (a d)"), ident)
            for i in range(TILES):
                pe.matmul(ps_y[0][:, i * PJ:(i + 1) * PJ], spread[:, i, :], wsit[:], start=True, stop=True)
            pe.matmul(ps_y[1][:, 0:PJ], ones[0:NF, :], wsit[:], start=True, stop=True).then_inc(pp, 1)
            pe.wait_ge(dp, 2)

            def shift_rows():
                pe.wait_ge(dw, 1)
                for c in range(FCH):
                    mm = pe.matmul(ps_b[0][0:BM, :], bmat[:, c, :], w_raw[:, c, :], start=(c == 0), stop=(c == FCH - 1))
                mm.then_inc(pw, 1)

            def shift_layer1():
                pe.wait_ge(s_w1, 16)
                for m in range(4):
                    for c in range(3):
                        mm = pe.matmul(ps_b[1][:, m:m + 1], w_raw[:, c, m * P:(m + 1) * P], bl[:, c:c + 1],
                                       start=(c == 0), stop=(c == 2))
                mm.then_inc(pw, 1)

            def turn_rows(s, n):
                it, c = divmod(n, 4)
                i0, i1 = CHUNKS[c]
                if after(s, n):
                    pe.wait_ge(d_prod, s * STEPS + n)
                for i in range(i0, i1):
                    pe.wait_ge(s_row[it % 2][i], 64 * s + 32 * (it // 2 + 1))
                    mm = pe.transpose(ps_t[:, (i - i0) * P:(i - i0 + 1) * P],
                                      emb[it % 2][:, i, :, :].rearrange("p g d -> p (g d)"), ident)
                mm.then_inc(s_tr, 1)

            def times_gram(s, n):
                i0, i1 = CHUNKS[n % 4]
                pe.wait_ge(a_tr, s * STEPS + n + 1)
                for i in range(i1 - i0):
                    mm = pe.matmul(ps_t[:, i * P:(i + 1) * P], embt[:, i * P:(i + 1) * P], gram2[:],
                                   start=True, stop=True)
                mm.then_inc(s_t, 1)

            def mix_features(s, n):
                pe.wait_ge(d_sc, s * STEPS + 8 + n + 1)
                if after(s, n):
                    pe.wait_ge(a_hi, s * 2 * STEPS + 2 * n)
                    pe.wait_ge(d_lo_u, s * 2 * STEPS + 2 * n)
                k = n % 4
                pieces = u_pieces(k)
                for m, (i, x, y) in enumerate(pieces):
                    f = first_sample(i)
                    mm = pe.matmul(ps_u[:, (x - BS * k) * PJ:(y - BS * k) * PJ],
                                   scaled[:, i, :, :].rearrange("p g d -> p (g d)"),
                                   mix[:, i, x - f:y - f, :].rearrange("p s q -> p (s q)"),
                                   start=(m == 0), stop=(m == len(pieces) - 1), skip_group_check=True)
                mm.then_inc(s_u, 1)

            def project(s, n, g):
                pe.wait_ge(a_hi, s * 2 * STEPS + 2 * n + g + 1)
                pe.wait_ge(d_lo_u, s * 2 * STEPS + 2 * n + g + 1)
                if after(s, n):
                    pe.wait_ge(d_t, s * 2 * STEPS + 2 * n + g - 1)
                pe.matmul(ps_y[g][:, :], wg_hi[:], upair[:, g, :], start=True, stop=False)
                pe.matmul(ps_y[g][:, :], wg_lo[:], ushift[:, g, :], start=False, stop=True).then_inc(s_y, 1)

            def gram_y(s, n, g):
                pe.wait_ge(d_x, s * STEPS + n + 1)
                pe.wait_ge(d_t, s * 2 * STEPS + 2 * n + g + 1)
                if after(s, n + g):
                    pe.wait_ge(a_z, s * 2 * STEPS + 2 * n + g)
                for t in range(4):
                    tv = tvec[:, n % 2, g, t, :]
                    mm = pe.matmul(ps_z[:, t // 2, (t % 2) * TW:(t % 2 + 1) * TW], tv[:, 0:4 * PJ], tv,
                                   start=True, stop=True)
                mm.then_inc(s_z, 1)

            def dense_turn(s, c):
                if c == 0:
                    pe.wait_ge(s_dense, 16 if isinstance(s, int) else 32 * s)
                if c == 0 and not isinstance(s, int):
                    pe.wait_ge(d_f, 6 * (s - 1) + 1)
                if c == 1 and not isinstance(s, int):
                    pe.wait_ge(a_yo, s)
                for j in range(4):
                    mm = pe.transpose(ps_b[1 - c][:, j * P:(j + 1) * P], dense[:, j, c * P:(c + 1) * P], ident)
                mm.then_inc(s_dt, 1)

            def dense_product(s, _):
                pe.wait_ge(d_dl, 2 * s + 2)
                for c in range(2):
                    mm = triple(ps_b[1][:, :], (wd_hi[:, c, :], wd_lo[:, c, :]), (d_hi[:, c, :], d_lo[:, c, :]),
                                c == 0, c == 1)
                mm.then_inc(s_xp, 1)

            def x_sums(s, _):
                pe.wait_ge(a_xs, s + 1)
                for j in range(4):
                    mm = pe.matmul(ps_b[0][:, j:j + 1], xa[:, j * P:(j + 1) * P], ones[:, 0:1], start=True, stop=True)
                mm.then_inc(s_xv, 1)

            def x_spread(s, _):
                pe.wait_ge(d_dg, s + 1)
                pe.matmul(ps_b[0][:, :], ones[:], xa[:], start=True, stop=True).then_inc(s_xs, 1)

            def sum_x(b, _):
                if not isinstance(b, int):
                    pe.wait_ge(a_h2, 2 * b)
                for j in range(4):
                    mm = pe.matmul(ps_b[1][:, j:j + 1], xt[:, j, :], ones[:, 0:1], start=True, stop=True)
                mm.then_inc(s_sx, 1)

            def turn_gram(b, q):
                if q == 0:
                    pe.wait_ge(a_z, 2 * STEPS * (b + 1))
                    pe.wait_ge(d_early, b + 1)
                    if isinstance(b, int):
                        pe.wait_ge(a_yo, b + 1)
                    else:
                        pe.wait_ge(d_xt, b + 2)
                elif q % 2:
                    pe.wait_ge(d_f, 6 * b + (q - 1) // 2 + 1)
                else:
                    pe.wait_ge(a_f, 5 * b + q // 2)
                for m in range(4):
                    mm = pe.transpose(ps_b[q % 2][:, m * P:(m + 1) * P], gram_all[:, 4 * q + m, :], ident)
                mm.then_inc(s_q, 1)

            def turn_feat(b, c):
                if c == 0:
                    pe.wait_ge(a_f, 5 * b + 5)
                    pe.wait_ge(d_f, 6 * b + 6)
                if c >= 2:
                    pe.wait_ge(d_fl, FCH * b + c - 1)
                for j in range(4):
                    mm = pe.transpose(ps_b[c % 2][:, j * P:(j + 1) * P], feat[:, j, c * P:(c + 1) * P], ident)
                mm.then_inc(s_ft, 1)

            def products(dst, count, first, last, operands, done):
                for at in range(first, last):
                    c, i = divmod(at, 3)
                    mm = pe.matmul(dst, *operands(c, i), start=(at == 0), stop=(at == count - 1))
                if last == count:
                    mm.then_inc(done, 1)

            def linear(b, j, first, last):
                if first == 0:
                    pe.wait_ge(d_fl, FCH * b + FCH)
                    if j >= 2:
                        pe.wait_ge(a_zn, 4 * b + j - 1)
                r = slice(j * P, (j + 1) * P)
                products(ps_b[1 - j % 2][:, :], 15, first, last,
                         lambda c, i: ((f_hi, f_hi, f_lo)[i][:, c, r], (wl_hi, wl_lo, wl_hi)[i][:, c, :]), s_o)

            def turn_dense(b, c):
                if c == 0:
                    pe.wait_ge(s_dense, 32 * b + 48 if not isinstance(b, int) else 32 * SUPERS)
                pe.wait_ge(a_zn, 4 * b + 3 + c)
                for j in range(4):
                    mm = pe.transpose(ps_b[1 - c][:, j * P:(j + 1) * P], dense[:, j, c * P:(c + 1) * P], ident)
                mm.then_inc(s_et, 1)

            def turn_z(b, c):
                if c < 2:
                    pe.wait_ge(d_el, 2 * b + c + 1)
                else:
                    pe.wait_ge(d_zl, 3 * b + 1)
                if c == 0:
                    pe.wait_ge(a_zn, 4 * b + 4)
                for j in range(4):
                    mm = pe.transpose(ps_b[1 - c % 2][:, j * P:(j + 1) * P], zn[:, j, c * P:(c + 1) * P], ident)
                mm.then_inc(s_zt, 1)

            def layer1(b, m, first, last):
                if first == 0:
                    if m < 2:
                        pe.wait_ge(d_zl, 3 * b + 3)
                    else:
                        pe.wait_ge(a_h1, 4 * b + m - 1)
                r = slice(m * P, (m + 1) * P)
                products(ps_b[m % 2][:, :], 15, first, last,
                         lambda c, i: ((w1_hi, w1_hi, w1_lo)[i][:, c, r],
                                       (z_hi, z_lo, z_hi)[i][:, c, :] if c < 3 else (d_hi, d_lo, d_hi)[i][:, c - 3, :]),
                         s_h1)

            def layer2(b, m, first, last):
                if first == 0:
                    pe.wait_ge(a_h1, 4 * b + 3 + m)
                if m == 0:
                    pe.wait_ge(d_h1l, 4 * b + min(4, (last - 1) // 3 + 1))
                r = slice(m * P, (m + 1) * P)
                products(ps_b[m][:, :], 12, first, last,
                         lambda c, i: ((w2_hi, w2_hi, w2_lo)[i][:, c, r], (h1_hi, h1_lo, h1_hi)[i][:, c, :]), s_h2)

            def layer3(b, _):
                for m in range(2):
                    pe.wait_ge(a_h2, 2 * b + m + 1)
                    mm = pe.matmul(ps_b[0][0:1, :], w3[:, m:m + 1], h2[:, m, :], start=(m == 0), stop=(m == 1))
                mm.then_inc(s_yo, 1)

            stage = {"dense_turn": dense_turn, "dense_product": dense_product, "x_sums": x_sums, "x_spread": x_spread,
                     "sum_x": sum_x, "turn_gram": turn_gram, "turn_feat": turn_feat, "linear": linear,
                     "turn_z": turn_z, "turn_dense": turn_dense, "layer1": layer1, "layer2": layer2, "layer3": layer3}

            def steps(s, b, count=STEPS):
                front = s if not isinstance(s, int) or s < SUPERS else None
                for n in range(count):
                    now, last, older = back_to(s, n), back_to(s, n - 1), back_to(s, n - 2)
                    if now:
                        turn_rows(*now)
                    run_slot(stage, 2 * n, front, b, False)
                    if now:
                        times_gram(*now)
                    if older:
                        gram_y(*older, 0)
                    if b is None and n == 3:
                        shift_rows()
                    if b is None and n == 10:
                        shift_layer1()
                    run_slot(stage, 2 * n + 1, front, b, False)
                    if last:
                        project(*last, 0)
                        project(*last, 1)
                    if older:
                        gram_y(*older, 1)
                    if now:
                        mix_features(*now)

            steps(0, None)
            pe.wait_ge(dw, 3)
            sum_x(0, 0)
            with pe.Fori(1, SUPERS) as s:
                steps(s, s - 1)
            steps(SUPERS, SUPERS - 1)

        @block.scalar
        def _(act):
            def copy(dst, src, done=None):
                ins = nc.scalar.activation(dst, src, ACT.Copy)
                if done is not None:
                    ins.then_inc(done, 1)

            def copy_turned(s, n):
                i0, i1 = CHUNKS[n % 4]
                w = (i1 - i0) * P
                act.wait_ge(s_tr, s * STEPS + n + 1)
                nc.scalar.activation(embt[:, 0:w], ps_t[:, 0:w], ACT.Copy).then_inc(a_tr, 1)

            def root_s(s, n):
                i0, i1 = CHUNKS[n % 4]
                w = 2 * (i1 - i0)
                act.wait_ge(d_var, s * STEPS + n + 1)
                nc.scalar.activation(std_s[:, 0:w], var_s[:, 0:w], ACT.Sqrt, bias=eps[:, 0:1],
                                     scale=1.0 / E).then_inc(a_std, 1)

            def u_high(s, n, g):
                act.wait_ge(s_u, s * STEPS + n + 1)
                nc.scalar.activation(upair[0:DS, g, :], ps_u[DS * g:DS * g + DS, :], ACT.Copy)
                nc.scalar.activation(ushift[0:DS, g, :], ps_u[DS * g:DS * g + DS, :], ACT.Copy).then_inc(a_hi, 1)

            def square_y(s, n, g):
                act.wait_ge(s_y, s * 2 * STEPS + 2 * n + g + 1)
                if after(s, n):
                    act.wait_ge(d_vy, s * 2 * STEPS + 2 * n + g - 1)
                nc.scalar.activation(ysq[:, g, :], ps_y[g][:, :], ACT.Square).then_inc(a_sq, 1)

            def root_y(s, n, g):
                act.wait_ge(d_vy, s * 2 * STEPS + 2 * n + g + 1)
                nc.scalar.activation(std_y[:, g, :], var_y[:, g, :], ACT.Sqrt, bias=eps[:, 0:1],
                                     scale=1.0 / PJ).then_inc(a_sdy, 1)

            def copy_gram(s, n, g):
                act.wait_ge(s_z, s * 2 * STEPS + 2 * n + g + 1)
                if n == EARLY and g == 0 and not isinstance(s, int):
                    act.wait_ge(s_q, (NG + 2) * s)
                if n < EARLY:
                    dst = gram_early[:, :, g, 4 * n:4 * n + 4]
                else:
                    dst = gram_all[:, :, gram_place(n, g):gram_place(n, g) + 4]
                src = ps_z[:, :, 0:2 * TW].rearrange("p b (t q) -> p b t q", t=2)
                for j in range(4):
                    r = slice(32 * j, 32 * j + 32)
                    nc.scalar.activation(dst[r, 0:PJ, :].rearrange("p q (b t) -> p b t q", b=2),
                                         src[r, :, :, PJ * j:PJ * (j + 1)], ACT.Copy)
                nc.scalar.activation(dst[:, PJ:PJ + 8, :].rearrange("p q (b t) -> p b t q", b=2),
                                     src[:, :, :, 4 * PJ:TW], ACT.Copy).then_inc(a_z, 1)

            def dense_turn(s, c):
                act.wait_ge(s_dt, 2 * s + c + 1)
                nc.scalar.activation(d_hi[:, c, :], ps_b[1 - c][:, :], ACT.Copy).then_inc(a_dh, 1)

            def dense_product(s, _):
                act.wait_ge(s_xp, s + 1)
                nc.scalar.activation(xa[:], ps_b[1][:, :], ACT.Square).then_inc(a_xs, 1)

            def x_sums(s, _):
                act.wait_ge(s_xv, s + 1)
                nc.scalar.activation(std_x[:], ps_b[0][:, 0:4], ACT.Sqrt, bias=eps[:, 0:1], scale=1.0 / E).then_inc(a_xd, 1)

            def turn_gram(b, q):
                if q % 2:
                    return
                act.wait_ge(s_q, (NG + 2) * b + q + 1)
                src = ps_b[0]
                if q < NG:
                    w = 4 * q + 3
                    dst = feat[:, :, OFF[q]:OFF[q] + 4 * w].rearrange("t j (m p) -> t m j p", m=4)
                    last = nc.scalar.activation(dst, src[:, :].rearrange("t (m j p) -> t m j p", m=4, j=4)[:, :, :, 0:w],
                                                ACT.Copy)
                else:
                    for j in range(2):
                        last = nc.scalar.activation(feat[:, j, XOFF:XOFF + 2 * PJ].rearrange("t (c p) -> t c p", c=2),
                                                    own_block(src, j), ACT.Copy)
                last.then_inc(a_f, 1)

            def turn_feat(b, c):
                act.wait_ge(s_ft, FCH * b + c + 1)
                nc.scalar.activation(f_hi[:, c, :], ps_b[c % 2][:, :], ACT.Copy).then_inc(a_fh, 1)

            def linear(b, j):
                act.wait_ge(d_ag, 4 * b + j + 1)
                nc.scalar.activation(std_o[:, j:j + 1], mv[:, j, 1:2], ACT.Sqrt, bias=eps[:, 0:1]).then_inc(a_sdo, 1)
                act.wait_ge(d_ro, 4 * b + j + 1)
                nc.scalar.activation(zn[:, j, :], ps_b[1 - j % 2][:, 0:KUSE], ACT.Copy,
                                     scale=rstd_o[:, j:j + 1]).then_inc(a_zn, 1)

            def turn_z(b, c):
                act.wait_ge(s_zt, 3 * b + c + 1)
                nc.scalar.activation(z_hi[:, c, :], ps_b[1 - c % 2][:, :], ACT.Copy).then_inc(a_zh, 1)

            def turn_dense(b, c):
                act.wait_ge(s_et, 2 * b + c + 1)
                nc.scalar.activation(d_hi[:, c, :], ps_b[1 - c][:, :], ACT.Copy).then_inc(a_eh, 1)

            def layer1(b, m):
                act.wait_ge(s_h1, 4 * b + m + 1)
                nc.scalar.activation(h1f[m], ps_b[m % 2][:, :], ACT.Relu, bias=b1z[:, m:m + 1]).then_inc(a_h1, 1)

            def layer2(b, m):
                act.wait_ge(s_h2, 2 * b + m + 1)
                nc.scalar.activation(h2[:, m, :], ps_b[m][:, :], ACT.Relu, bias=b2[:, m:m + 1]).then_inc(a_h2, 1)

            def layer3(b, _):
                act.wait_ge(s_yo, b + 1)
                act.wait_ge(s_yfree, b + 1)
                nc.scalar.activation(yrow[0:1, :].rearrange("o (t j) -> o t j", j=4),
                                     ps_b[0][0:1, :].rearrange("o (j t) -> o t j", j=4), ACT.Copy).then_inc(a_yo, 1)

            stage = {"dense_turn": dense_turn, "dense_product": dense_product, "x_sums": x_sums,
                     "turn_gram": turn_gram, "turn_feat": turn_feat, "linear": linear, "turn_z": turn_z,
                     "turn_dense": turn_dense, "layer1": layer1, "layer2": layer2, "layer3": layer3}

            def steps(s, b, count=STEPS):
                front = s if not isinstance(s, int) or s < SUPERS else None
                for n in range(count):
                    now, last, older = back_to(s, n), back_to(s, n - 1), back_to(s, n - 2)
                    if now:
                        copy_turned(*now)
                    if last:
                        u_high(*last, 0)
                        u_high(*last, 1)
                    if older:
                        copy_gram(*older, 0)
                    if now:
                        root_s(*now)
                    run_slot(stage, 2 * n, front, b, True)
                    if last:
                        square_y(*last, 0)
                        square_y(*last, 1)
                    run_slot(stage, 2 * n + 1, front, b, True)
                    if last:
                        root_y(*last, 0)
                    if older:
                        copy_gram(*older, 1)
                    if last:
                        root_y(*last, 1)

            act.sem_inc(a_yo, 1)
            act.sem_inc(s_yfree, 1)
            act.wait_ge(dp, 2)
            steps(0, None)
            with act.Fori(1, SUPERS) as s:
                steps(s, s - 1)
            steps(SUPERS, SUPERS - 1)

        @block.vector
        def _(dve):
            V = nc.vector
            chain = [0]

            def link(ins):
                chain[0] += 1
                ins.then_inc(s_chain, 1)
                dve.wait_ge(s_chain, chain[0])

            def pair(hi, lo, src):
                link(V.tensor_copy(hi, src))
                return V.tensor_tensor(lo, src, hi.bitcast(F32), ALU.subtract)

            dve.sem_inc(d_sc, 8)
            V.memset(ones[:], 1.0).then_inc(s_chain, 1)
            V.memset(eps[:], EPS).then_inc(s_chain, 1)
            V.memset(tvec[:], 1.0).then_inc(s_chain, 1)
            chain[0] = 3
            dve.wait_ge(s_const, 16 * 6)
            dve.wait_ge(pp, 1)
            for g in range(2):
                link(V.tensor_copy(wsc2[:, g, :], ps_t[:, 0:DS]))
            link(V.tensor_scalar(wg2[:], wsc2[:], gs[:, 0:1], None, ALU.mult))
            link(V.tensor_copy(wd_hi[:].rearrange("p c e -> p (c e)"), ps_u[:, 0:DD]))
            link(V.tensor_tensor(wd_lo[:].rearrange("p c e -> p (c e)"), ps_u[:, 0:DD],
                                 wd_hi[:].rearrange("p c e -> p (c e)").bitcast(F32), ALU.subtract))
            V.tensor_copy(wsit[:], ps_y[0][0:NF, 0:PJ]).then_inc(dp, 1)
            dve.wait_ge(pp, 2)
            link(V.tensor_tensor(gram2[:], ps_t[:, 0:P], blockmask, ALU.mult))
            link(V.tensor_copy(wg_hi[:], ps_u[:, 0:P]))
            H = slice(DS, P)
            link(V.tensor_tensor(wg_lo[0:DS], ps_u[0:DS, 0:P], wg_hi[0:DS].bitcast(F32), ALU.subtract))
            split(link, V, shift_t[H, 0, :], wg_lo[H], bsr[H, :], shift_t[H, 1, :], shift_t[H, 2, :],
                  rowmask[H, 0:1], rowmask[H, 1:2])
            link(V.tensor_copy(shift_t[H, 0, 0:PJ], ps_y[1][H, 0:PJ]))
            split(link, V, shift_t[H, 0, 0:PJ], ushift[H, 0, 0:PJ], shift_t[H, 0, 0:PJ], shift_t[H, 1, 0:PJ],
                  shift_t[H, 2, 0:PJ], rowmask[H, 2:3], rowmask[H, 3:4])
            link(V.tensor_copy(shift_t[H, 0, 0:PJ], ushift[H, 0, 0:PJ].bitcast(F32)))
            for g in range(2):
                link(V.tensor_copy(ushift[H, g, :].rearrange("p (s q) -> p s q", q=PJ),
                                   shift_t[H, 0, 0:PJ].unsqueeze(1).to_broadcast([DS, BS, PJ])))
            for w in range(WINDOW):
                ins = V.tensor_tensor(mix[:, :, w, :], ps_y[0][:, 0:TILES * PJ].rearrange("p (i q) -> p i q", q=PJ),
                                      window[:, :, w:w + 1].to_broadcast([P, TILES, PJ]), ALU.mult)
                ins.then_inc(s_chain, 1)
            chain[0] += WINDOW
            dve.wait_ge(s_chain, chain[0])
            V.memset(var_s[:], 0.0).then_inc(dp, 1)

            def shift_matrix():
                dve.wait_ge(s_wl, 32)
                lo = ROFF - 4 * P
                link(V.memset(bmat, 0.0))
                for c in range(FCH):
                    link(V.tensor_scalar(bmat[:, c, lo:lo + QC], ind_p[:, c, :], bb[:, c:c + 1], None, ALU.mult))
                    link(V.scalar_tensor_tensor(bmat[:, c, lo:lo + QC], ind_q[:, c, :], ba[:, c:c + 1],
                                                bmat[:, c, lo:lo + QC], ALU.mult, ALU.add))
                    ins = V.tensor_scalar(bmat[:, c, lo + QC - 1:lo + QC], ba[:, c:c + 1], bb[:, c:c + 1], float(E),
                                          ALU.mult, ALU.mult)
                    if c < FCH - 1:
                        link(ins)
                ins.then_inc(dw, 1)

            def weights_linear(c):
                if c == 0:
                    dve.wait_ge(pw, 1)
                row = w_raw[:, c, :]
                link(V.tensor_scalar(row, row, ga[:, c:c + 1], gb[:, c:c + 1], ALU.mult, ALU.mult))
                if c == FCH - 1:
                    link(V.scalar_tensor_tensor(row[0:BM], ps_b[0][0:BM, :], gr[0:BM, 0:1], row[0:BM],
                                                ALU.mult, ALU.add))
                link(V.tensor_reduce(std_o[:, 0:1], row, AX.X, ALU.add))
                link(V.tensor_scalar(std_o[:, 1:2], std_o[:, 0:1], -1.0 / KOUT, None, ALU.mult))
                link(V.tensor_scalar(row, row, std_o[:, 1:2], None, ALU.add))
                ins = pair(wl_hi[:, c, :], wl_lo[:, c, :], row)
                if c == FCH - 1:
                    ins.then_inc(dw, 1)

            def weights_layer1(c):
                if c == 0:
                    dve.wait_ge(pw, 2)
                    link(V.tensor_tensor(b1z[:], ps_b[1][:, 0:4], b1, ALU.add))
                if c < 3:
                    link(V.tensor_scalar(w_raw[:, c, :], w_raw[:, c, :], gl[:, c:c + 1], None, ALU.mult))
                link(pair(w1_hi[:, c, :], w1_lo[:, c, :], w_raw[:, c, :]))

            def weights_layer2():
                dve.wait_ge(s_w2, 16)
                link(pair(w2_hi[:], w2_lo[:], w2_raw))
                link(V.memset(feat[:, :, ONEOFF:FEAT], 0.0))
                V.memset(feat[:, :, ONEOFF:ONEOFF + 1], 1.0).then_inc(dw, 1)

            def u_low(s, n, g):
                dve.wait_ge(a_hi, s * 2 * STEPS + 2 * n + g + 1)
                V.tensor_tensor(upair[DS:P, g, :], ps_u[DS * g:DS * g + DS, :],
                                upair[0:DS, g, :].bitcast(F32), ALU.subtract).then_inc(d_lo_u, 1)

            def variance_s(s, n):
                it, c = divmod(n, 4)
                i0, i1 = CHUNKS[c]
                w = 2 * (i1 - i0)
                dve.wait_ge(s_t, s * STEPS + n + 1)
                V.tensor_tensor(prod[:, 0:w, :], ps_t[:, 0:w * DS].rearrange("p (w d) -> p w d", d=DS),
                                emb[it % 2][:, i0:i1, :, :].rearrange("p i g d -> p (i g) d"),
                                ALU.mult).then_inc(d_prod, 1)
                dve.wait_ge(d_prod, s * STEPS + n + 1)
                V.tensor_reduce(var_s[:, 0:w], prod[:, 0:w, :], AX.X, ALU.add).then_inc(d_var, 1)

            def scale_s(s, n):
                it, c = divmod(n, 4)
                i0, i1 = CHUNKS[c]
                w = 2 * (i1 - i0)
                dve.wait_ge(a_std, s * STEPS + n + 1)
                V.reciprocal(rstd_s[:, 0:w], std_s[:, 0:w]).then_inc(d_rs, 1)
                dve.wait_ge(d_rs, s * STEPS + n + 1)
                V.tensor_tensor(scaled[:, i0:i1, :, :].rearrange("p i g d -> p (i g) d"),
                                emb[it % 2][:, i0:i1, :, :].rearrange("p i g d -> p (i g) d"),
                                rstd_s[:, 0:w].unsqueeze(2).to_broadcast([P, w, DS]), ALU.mult).then_inc(d_sc, 1)

            def variance_y(s, n, g):
                dve.wait_ge(a_sq, s * 2 * STEPS + 2 * n + g + 1)
                V.tensor_reduce(var_y[:, g, :], ysq[:, g, :].rearrange("p (s q) -> p s q", q=PJ), AX.X,
                                ALU.add).then_inc(d_vy, 1)

            def norm_y(s, n, g):
                dve.wait_ge(a_sdy, s * 2 * STEPS + 2 * n + g + 1)
                V.reciprocal(rstd_y[:, g, :], std_y[:, g, :]).then_inc(d_ry, 1)
                dve.wait_ge(d_ry, s * 2 * STEPS + 2 * n + g + 1)
                V.tensor_tensor(tvec[:, n % 2, g, :, 0:4 * PJ].rearrange("p t (j q) -> p t j q", j=4),
                                ps_y[g][:, :].rearrange("p (t j q) -> p t j q", t=4, j=4),
                                rstd_y[:, g, :].rearrange("p (t j) -> p t j", t=4).unsqueeze(3).to_broadcast(
                                    [P, 4, 4, PJ]), ALU.mult).then_inc(d_t, 1)

            def x_column(s, n):
                if n == 0:
                    dve.wait_ge(d_xt, s + 1)
                if after(s, n, 2):
                    dve.wait_ge(s_z, s * 2 * STEPS + 2 * n - 2)
                for g in range(2):
                    t0 = gram_place(n, g)
                    last = V.tensor_copy(tvec[:, n % 2, g, :, 4 * PJ:TW:2],
                                         xt[:, :, t0:t0 + 4].rearrange("p j t -> p t j"))
                last.then_inc(d_x, 1)

            def dense_turn(s, c):
                dve.wait_ge(a_dh, 2 * s + c + 1)
                V.tensor_tensor(d_lo[:, c, :], ps_b[1 - c][:, :], d_hi[:, c, :].bitcast(F32),
                                ALU.subtract).then_inc(d_dl, 1)

            def x_sums(s, _):
                dve.wait_ge(a_xd, s + 1)
                V.reciprocal(rstd_x[:], std_x[:]).then_inc(d_xr, 1)
                dve.wait_ge(d_xr, s + 1)
                V.tensor_tensor(xa[:].rearrange("p (j t) -> p j t", j=4), ident.unsqueeze(1).to_broadcast([P, 4, P]),
                                rstd_x[:].unsqueeze(2).to_broadcast([P, 4, P]), ALU.mult).then_inc(d_dg, 1)

            def x_spread(s, _):
                dve.wait_ge(s_xs, s + 1)
                V.tensor_copy(xb[:], ps_b[0][:, :]).then_inc(d_xr2, 1)
                dve.wait_ge(d_xr2, s + 1)
                V.tensor_tensor(xb[:], ps_b[1][:, :], xb[:], ALU.mult).then_inc(d_xn, 1)
                dve.wait_ge(d_xn, s + 1)
                V.tensor_scalar(xt[:].rearrange("p j t -> p (j t)"), xb[:], gd[:, 0:1], bd[:, 0:1],
                                ALU.mult, ALU.add).then_inc(d_xt, 1)

            def move_early(s, _):
                if not isinstance(s, int):
                    dve.wait_ge(s_q, (NG + 2) * s)
                dve.wait_ge(a_z, 2 * STEPS * s + 2 * EARLY)
                V.tensor_copy(gram_all[:, :, 0:32].rearrange("p q (g t) -> p q g t", g=2)[:, :, :, 0:4 * EARLY],
                              gram_early[:]).then_inc(d_early, 1)

            def sum_x(b, _):
                dve.wait_ge(s_sx, b + 1)
                V.tensor_copy(feat[:, :, SXOFF:SXOFF + 1].rearrange("t j o -> t (j o)"), ps_b[1][:, 0:4]).then_inc(d_f, 1)

            def turn_gram(b, q):
                if q % 2 == 0:
                    return
                dve.wait_ge(s_q, (NG + 2) * b + q + 1)
                if q < NG:
                    w = 4 * q + 3
                    last = V.tensor_copy(feat[:, :, OFF[q]:OFF[q] + 4 * w].rearrange("t j (m p) -> t m j p", m=4),
                                         ps_b[1][:, :].rearrange("t (m j p) -> t m j p", m=4, j=4)[:, :, :, 0:w])
                else:
                    for j in range(2, 4):
                        last = V.tensor_copy(feat[:, j, XOFF:XOFF + 2 * PJ].rearrange("t (c p) -> t c p", c=2),
                                             own_block(ps_b[1], j))
                last.then_inc(d_f, 1)

            def turn_feat(b, c):
                dve.wait_ge(a_fh, FCH * b + c + 1)
                V.tensor_tensor(f_lo[:, c, :], ps_b[c % 2][:, :], f_hi[:, c, :].bitcast(F32),
                                ALU.subtract).then_inc(d_fl, 1)

            def linear(b, j):
                dve.wait_ge(s_o, 4 * b + j + 1)
                V.bn_stats(stats[:, j, :], ps_b[1 - j % 2][:, :]).then_inc(d_bn, 1)
                dve.wait_ge(d_bn, 4 * b + j + 1)
                dve.sem_inc(s_seen, 1)
                V.bn_aggr(mv[:, j, :], stats[:, j, :]).then_inc(d_ag, 1)
                dve.wait_ge(a_sdo, 4 * b + j + 1)
                V.reciprocal(rstd_o[:, j:j + 1], std_o[:, j:j + 1]).then_inc(d_ro, 1)

            def turn_z(b, c):
                dve.wait_ge(a_zh, 3 * b + c + 1)
                V.tensor_tensor(z_lo[:, c, :], ps_b[1 - c % 2][:, :], z_hi[:, c, :].bitcast(F32),
                                ALU.subtract).then_inc(d_zl, 1)

            def turn_dense(b, c):
                dve.wait_ge(a_eh, 2 * b + c + 1)
                V.tensor_tensor(d_lo[:, c, :], ps_b[1 - c][:, :], d_hi[:, c, :].bitcast(F32),
                                ALU.subtract).then_inc(d_el, 1)

            def layer1(b, m):
                dve.wait_ge(a_h1, 4 * b + m + 1)
                V.tensor_copy(h1_hi[:, m, :], h1f[m]).then_inc(d_h1h, 1)
                dve.wait_ge(d_h1h, 4 * b + m + 1)
                V.tensor_tensor(h1_lo[:, m, :], h1f[m], h1_hi[:, m, :].bitcast(F32), ALU.subtract).then_inc(d_h1l, 1)

            stage = {"dense_turn": dense_turn, "x_sums": x_sums, "x_spread": x_spread, "move_early": move_early,
                     "sum_x": sum_x, "turn_gram": turn_gram, "turn_feat": turn_feat, "linear": linear,
                     "turn_z": turn_z, "turn_dense": turn_dense, "layer1": layer1}

            def steps(s, b, count=STEPS):
                front = s if not isinstance(s, int) or s < SUPERS else None
                for n in range(count):
                    now, last = back_to(s, n), back_to(s, n - 1)
                    if last:
                        u_low(*last, 0)
                    if now:
                        variance_s(*now)
                    if last:
                        u_low(*last, 1)
                    if now:
                        scale_s(*now)
                    run_slot(stage, 2 * n, front, b, True)
                    if last:
                        variance_y(*last, 0)
                        variance_y(*last, 1)
                    run_slot(stage, 2 * n + 1, front, b, True)
                    if b is None:
                        if n == 2:
                            shift_matrix()
                        if 4 <= n <= 8:
                            weights_linear(n - 4)
                        if 11 <= n <= 15:
                            weights_layer1(n - 11)
                        if n == 15:
                            weights_layer2()
                    if last:
                        x_column(*last)
                        norm_y(*last, 0)
                        norm_y(*last, 1)

            steps(0, None)
            sum_x(0, 0)
            with dve.Fori(1, SUPERS) as s:
                steps(s, s - 1)
            steps(SUPERS, SUPERS - 1)


def split(link, V, tmp, dst, src, hi, lo, take_hi, take_lo):
    link(V.tensor_copy(dst, src))
    link(V.tensor_copy(hi, dst.bitcast(F32)))
    link(V.tensor_tensor(lo, src, hi, ALU.subtract))
    link(V.tensor_scalar(hi, hi, take_hi, None, ALU.mult))
    link(V.scalar_tensor_tensor(dst, lo, take_lo, hi, ALU.mult, ALU.add))


def constants():
    r = np.arange(P)
    c = {}
    row = P * np.arange(TILES)[None, :] + r[:, None]
    c["c_spread"] = (np.arange(NF)[:, None, None] == (row % NF).T[None])
    first = np.array([first_sample(i) for i in range(TILES)])
    window = (row // NF - first)[:, :, None] == np.arange(WINDOW)
    c["c_big"] = np.concatenate([np.eye(P), np.eye(P) - 1.0 / E, np.kron(np.eye(2), np.ones((DS, DS))),
                                 window.reshape(P, -1)], axis=1)
    p, q, col = feature_map()
    ip, iq = np.zeros((FEAT, QC)), np.zeros((FEAT, QC))
    for f in range(FEAT):
        if q[f] >= 0:
            ip[f, p[f]] = 1
            iq[f, q[f]] = 1
        elif p[f] >= 0:
            iq[f, PJ] = 1
    c["c_inds"] = np.stack([ip, iq]).reshape(2, FCH, P, QC).transpose(2, 0, 1, 3)
    return {k: np.ascontiguousarray(v, dtype=np.float32) for k, v in c.items()}


def feature_map():
    p, q, col = (np.full(FEAT, -1) for _ in range(3))
    for g in range(NG):
        w = 4 * g + 3
        for m in range(4):
            for x in range(w):
                y = 4 * g + m
                if x < y:
                    f = OFF[g] + m * w + x
                    p[f], q[f], col[f] = x, y, (y + 1) * y // 2 + x + 1
    for x in range(PJ):
        p[XOFF + x], col[XOFF + x] = x, (x + 1) * x // 2
    return p, q, col


def kernel(**inputs):
    import concourse.bacc as _bacc
    from concourse.bass_utils import run_bass_kernel_spmd as _run

    x = {k: np.asarray(v) for k, v in inputs.items()}
    table = np.concatenate([x[f"tbl_{f}"] for f in range(NF)], axis=0)
    begin = np.cumsum([0] + [x[f"tbl_{f}"].shape[0] for f in range(NF - 1)])
    row = P * np.arange(TILES)[None, :] + np.arange(P)[:, None]
    p, q, col = feature_map()

    def place(v, where, none):
        full = np.full((FEAT,) + v.shape[1:], none, np.float32)
        full[where >= 0] = v[where[where >= 0]]
        return np.ascontiguousarray(full.reshape((FCH, P) + v.shape[1:]).swapaxes(0, 1))

    def cols(v, n):
        return np.ascontiguousarray(v.reshape(n, P).T)

    gsi, bsi = x["L0_rec_gsi"], x["L0_rec_bsi"]
    gr = np.zeros((P, 1), np.float32)
    gr[ROFF - 4 * P:ROFF - 4 * P + PJ, 0] = gsi
    gr[SXOFF - 4 * P:ONEOFF - 4 * P + 1, 0] = 1.0
    rowmask = np.zeros((P, 4), np.float32)
    rowmask[DS:DS + 4] = [[1, 0, 1, 0], [1, 0, 0, 1], [0, 1, 1, 0], [0, 1, 0, 1]]
    vectors = {"gs": x["L0_rec_gs"].reshape(P, 1), "gd": x["L0_rec_gd"].reshape(P, 1),
               "bd": x["L0_rec_bd"].reshape(P, 1), "gr": gr, "ga": place(gsi, p, 1.0), "gb": place(gsi, q, 1.0),
               "ba": place(bsi, p, 0.0), "bb": place(bsi, q, 0.0), "gl": cols(x["L0_rec_gl"][:KUSE], 3),
               "bl": cols(x["L0_rec_bl"][:KUSE], 3), "b1": cols(x["b_top1"], 4), "b2": cols(x["b_top2"], 2),
               "w3": cols(x["W_top3"], 2), "rowmask": rowmask}
    w1 = x["W_top1"].reshape(6, P, H1)
    arrays = {
        "table": table,
        "ids": np.ascontiguousarray(x["ids"].reshape(-1, P).T).reshape(P, ITERS * SUPERS, 2, TILES),
        "c_base": np.ascontiguousarray(begin[row % NF].astype(np.int32)),
        "dense": np.ascontiguousarray(x["r_dense_t"]).reshape(SUPERS * P, 4, DD),
        "Wsd": np.concatenate([x["L0_rec_Ws"], x["L0_rec_Wd"]], axis=1),
        "small": np.concatenate([(np.eye(PJ) - 1.0 / PJ).astype(np.float32), x["L0_rec_Wsi"]], axis=1),
        "bs": x["L0_rec_bs"].reshape(1, P),
        "vecs": np.concatenate([vectors[name] for name in VECS], axis=1),
        "Wl": place(x["L0_rec_Wl"].T, col, 0.0),
        "W1": np.ascontiguousarray(w1[[0, 1, 2, 4, 5]].transpose(1, 0, 2)),
        "W2": np.ascontiguousarray(x["W_top2"].reshape(4, P, H2).transpose(1, 0, 2)),
        **constants(),
    }
    nc = _bacc.Bacc("TRN2", target_bir_lowering=False, num_devices=1)
    a, feed = {}, {}
    for name, v in arrays.items():
        v = np.ascontiguousarray(v)
        feed[f"in_{name}"] = v
        a[name] = nc.dram_tensor(f"in_{name}", v.shape, mybir.dt.from_np(v.dtype), kind="ExternalInput").ap()
    out = nc.dram_tensor("out_y", (SUPERS, SUPER), F32, kind="ExternalOutput").ap()
    build(nc, a, out)
    r = _run(nc, [feed], core_ids=[0])
    return r.results[0]["out_y"].reshape(BATCH, 1)
```

```python
from contextlib import ExitStack

import numpy as np
import concourse.bass as bass
from concourse import mybir

F32 = mybir.dt.float32
F32R = mybir.dt.float32r
I32 = mybir.dt.int32
ALU = mybir.AluOpType
ACT = mybir.ActivationFunctionType
AX = mybir.AxisListType

P = 128
NF = 26
DS = 64
E = 128
PJ = 32
DD = 256
KOUT = 512
KUSE = 384
H1, H2 = 512, 256
EPS = 1e-5
BATCH = 2048
SUPERS = 4
ITERS = 4
SUPER = BATCH // SUPERS
GROUP = 64
TILES = GROUP * NF // P
CHUNKS = [(0, 4), (4, 7), (7, 10), (10, 13)]
STEPS = ITERS * len(CHUNKS)
BS = GROUP // 4
QC = PJ + 2
TW = 4 * PJ + 8
NG = PJ // 4
OFF = [sum(4 * (4 * h + 3) for h in range(g)) for g in range(NG + 1)]
XOFF, ROFF, SXOFF, ONEOFF = OFF[NG], OFF[NG] + PJ, OFF[NG] + 2 * PJ, OFF[NG] + 2 * PJ + 1
FCH = 5
FEAT = FCH * P
WINDOW = 6
BM = ONEOFF - 4 * P + 1
VECS, VN = {}, 0
for _name, _n in (("gs", 1), ("gd", 1), ("bd", 1), ("gr", 1), ("ga", FCH), ("gb", FCH), ("ba", FCH), ("bb", FCH),
                  ("gl", 3), ("bl", 3), ("b1", 4), ("b2", 2), ("w3", 2), ("rowmask", 4)):
    VECS[_name] = (VN, _n)
    VN += _n


def first_sample(i):
    return P * i // NF


def last_sample(i):
    return (P * i + P - 1) // NF


def u_pieces(k):
    out = []
    for i in range(TILES):
        a, b = max(first_sample(i), BS * k), min(last_sample(i) + 1, BS * (k + 1))
        if a < b:
            out.append((i, a, b))
    return out


def parts(name, last, each, slots):
    total, out, at = last * each, [], 0
    for i in range(len(slots)):
        end = total * (i + 1) // len(slots)
        items = []
        while at < end:
            k = at // each
            stop = min(end, (k + 1) * each)
            items.append((name, k, at - k * each, stop - k * each))
            at = stop
        out.append((slots[i], items))
    return out


SLOTS = [[] for _ in range(2 * STEPS)]
for _at, _items in ([(0, [("dense_turn", 0), ("dense_turn", 1)]), (1, [("dense_product", 0)]),
                     (2, [("x_sums", 0)]), (3, [("x_spread", 0)]),
                     (4, [("turn_gram", 0), ("turn_gram", 1)]), (5, [("turn_gram", 2), ("turn_gram", 3)]),
                     (6, [("turn_gram", 4), ("turn_gram", 5)]), (7, [("turn_gram", 6), ("turn_gram", 7)]),
                     (8, [("turn_gram", 8), ("turn_gram", 9)]), (9, [("turn_dense", 0), ("turn_dense", 1)]),
                     (10, [("turn_feat", 0), ("turn_feat", 1)]), (11, [("turn_feat", 2), ("turn_feat", 3)]),
                     (12, [("turn_feat", 4)])]
                    + parts("linear", 4, 15, range(12, 20))
                    + [(21, [("turn_z", 0), ("turn_z", 1)]), (22, [("turn_z", 2)])]
                    + parts("layer1", 4, 15, range(22, 28)) + parts("layer2", 2, 12, range(28, 31))
                    + [(31, [("layer3", 0), ("sum_x", 0)])]):
    SLOTS[_at] += _items
OF_THIS_SUPER = ("sum_x", "dense_turn", "dense_product", "x_sums", "x_spread", "move_early")
EARLY = 3
PRODUCTS = {"linear": 15, "layer1": 15, "layer2": 12}


def readers(late):
    slots = [[] for _ in range(2 * STEPS)]
    for at, items in enumerate(SLOTS):
        for name, k, *cut in items:
            for part, (stage, by) in late.items():
                if stage == name and (not cut or cut[1] == PRODUCTS[name]):
                    slots[at + by].append((part, k))
    return slots


def run_slot(stage, slots, at, s, b):
    for name, *args in slots[at]:
        if name == "sum_x" and b is None:
            continue
        of = s if name in OF_THIS_SUPER else b
        if of is not None:
            stage[name](of, *args)


def after(s, n, k=1):
    return not isinstance(s, int) or STEPS * s + n >= k


def back_to(s, n):
    if n >= 0:
        return (s, n) if not isinstance(s, int) or s < SUPERS else None
    if isinstance(s, int) and s == 0:
        return None
    return (s - 1, n + STEPS)


def build(nc, a, out):
    ctx = ExitStack()
    with ctx:
        def sb(name, shape, dt=F32):
            return ctx.enter_context(nc.sbuf_tensor(name, shape, dt))

        def psum(name, shape):
            return ctx.enter_context(nc.psum_tensor(name, shape, F32))

        def sem(name):
            return ctx.enter_context(nc.semaphore(name))

        ps_t = psum("ps_t", [P, 512])
        ps_u = psum("ps_u", [P, 512])
        ps_y = [psum(f"ps_y{g}", [P, 512]) for g in range(2)]
        ps_z = psum("ps_z", [P, 2, 512])
        ps_b = [psum(f"ps_b{i}", [P, 512]) for i in range(2)]

        big = sb("big", [P, 3 * P + TILES * WINDOW])
        ident, center, blockmask = big[:, 0:P], big[:, P:2 * P], big[:, 2 * P:3 * P]
        window = big[:, 3 * P:].rearrange("p (i w) -> p i w", w=WINDOW)
        small = sb("small", [PJ, PJ + NF])
        center_p, wsi = small[:, 0:PJ], small[:, PJ:PJ + NF]
        inds = sb("inds", [P, 2, FCH, QC])
        ind_p, ind_q = inds[:, 0], inds[:, 1]
        vecs = sb("vecs", [P, VN])

        def vec(name):
            at, n = VECS[name]
            return vecs[:, at:at + n]

        gs, gd, bd, gr = vec("gs"), vec("gd"), vec("bd"), vec("gr")
        ga, gb, ba, bb = vec("ga"), vec("gb"), vec("ba"), vec("bb")
        gl, bl, b1, b2, w3, rowmask = vec("gl"), vec("bl"), vec("b1"), vec("b2"), vec("w3"), vec("rowmask")
        ones = sb("ones", [P, P])
        eps = sb("eps", [P, 1])
        wsd = sb("wsd", [P, DS + DD])
        ws, wd = wsd[:, 0:DS], wsd[:, DS:DS + DD]
        bsr = sb("bsr", [P, E])
        wsc2 = sb("wsc2", [P, 2, DS])
        wg2 = sb("wg2", [P, 2, DS])
        gram2 = sb("gram2", [P, P])
        wg_hi, wg_lo = sb("wg_hi", [P, E], F32R), sb("wg_lo", [P, E], F32R)
        wsit = sb("wsit", [NF, PJ])
        mix = sb("mix", [P, TILES, WINDOW, PJ])
        wd_hi, wd_lo = sb("wd_hi", [P, 2, E], F32R), sb("wd_lo", [P, 2, E], F32R)
        wl_hi, wl_lo = sb("wl_hi", [P, FCH, KOUT], F32R), sb("wl_lo", [P, FCH, KOUT], F32R)
        w1_hi, w1_lo = sb("w1_hi", [P, 5, H1], F32R), sb("w1_lo", [P, 5, H1], F32R)
        w2_hi, w2_lo = sb("w2_hi", [P, 4, H2], F32R), sb("w2_lo", [P, 4, H2], F32R)
        b1z = sb("b1z", [P, 4])

        ids = sb("ids", [P, ITERS * SUPERS, 2, TILES], I32)
        base = sb("base", [P, TILES], I32)
        rows_now = [sb(f"rows_now{i}", [P, 2, TILES], I32) for i in range(ITERS)]
        emb = [sb(f"emb{i}", [P, TILES, 2, DS]) for i in range(2)]
        scaled = sb("scaled", [P, TILES, 2, DS])
        embt = sb("embt", [P, 4 * P])
        prod = sb("prod", [P, 8, DS])
        var_s, std_s, rstd_s = sb("var_s", [P, 8]), sb("std_s", [P, 8]), sb("rstd_s", [P, 8])
        upair = sb("upair", [P, 2, 512], F32R)
        ushift = sb("ushift", [P, 2, 512], F32R)
        ysq = sb("ysq", [P, 2, 512])
        var_y, std_y, rstd_y = sb("var_y", [P, 2, BS]), sb("std_y", [P, 2, BS]), sb("rstd_y", [P, 2, BS])
        tvec = sb("tvec", [P, 2, 2, 4, TW])
        gram_all, gram_early = sb("gram_all", [P, PJ + 8, P]), sb("gram_early", [P, PJ + 8, 2, 4 * EARLY])

        dense = sb("dense", [P, 4, DD])
        d_hi, d_lo = sb("d_hi", [P, 2, 512], F32R), sb("d_lo", [P, 2, 512], F32R)
        xa, xb = sb("xa", [P, 512]), sb("xb", [P, 512])
        std_x, rstd_x = sb("std_x", [P, 4]), sb("rstd_x", [P, 4])
        xt = sb("xt", [P, 4, P])
        feat = sb("feat", [P, 4, FEAT])
        f_hi, f_lo = sb("f_hi", [P, FCH, 512], F32R), sb("f_lo", [P, FCH, 512], F32R)
        stats, mv = sb("stats", [P, 4, 6]), sb("mv", [P, 4, 2])
        std_o, rstd_o = sb("std_o", [P, 4]), sb("rstd_o", [P, 4])
        zn = sb("zn", [P, 4, KUSE])
        z_hi, z_lo = sb("z_hi", [P, 3, 512], F32R), sb("z_lo", [P, 3, 512], F32R)
        yrow = sb("yrow", [1, 512])
        shift_t = prod[:].rearrange("p w d -> p (w d)").rearrange("p (k e) -> p k e", k=4)
        w_raw = feat[:].rearrange("p j f -> p (j f)").rearrange("p (c m) -> p c m", c=5)
        zn_flat = zn[:].rearrange("p j k -> p (j k)")
        w2_raw = zn_flat[:, 0:4 * H2].rearrange("p (c m) -> p c m", c=4)
        bmat = zn_flat[:, 4 * H2:4 * H2 + FCH * BM].rearrange("p (c m) -> p c m", c=FCH)
        spread = scaled[0:NF].rearrange("p i g d -> p i (g d)")
        h1_hi, h1_lo = f_hi[:, 0:4, :], f_lo[:, 0:4, :]
        h2 = zn_flat[:, 0:2 * 512].rearrange("p (m b) -> p m b", m=2)
        h1f = [feat[:, m, 0:512] for m in range(4)]

        s_ids, s_dense, s_out = sem("ids_loaded"), sem("dense_loaded"), sem("out_stored")
        s_const, s_vecs, s_wl, s_w1, s_w2 = (sem("front_weights_loaded"), sem("vectors_loaded"), sem("wl_loaded"),
                                             sem("w1_loaded"), sem("w2_loaded"))
        s_idx, s_now = sem("row_numbers_ready"), sem("rows_now_ready")
        s_seen = sem("wait_carrier")
        s_row = [[sem(f"rows_landed_{b}_{i}") for i in range(TILES)] for b in range(2)]
        pp, dp, pw, dw, s_chain = (sem("prep_pe"), sem("prep_dve"), sem("back_weights_pe"), sem("back_weights_dve"),
                                   sem("prep_chain"))
        aw, a_wh, d_wc = sem("weights_scaled"), sem("weights_high"), sem("weights_centred")
        s_tr, s_t, s_u, s_y, s_z = sem("embt_done"), sem("t_done"), sem("u_done"), sem("y_done"), sem("gram_done")
        s_dt, s_xp, s_xv, s_xs = sem("dense_turned"), sem("x_product"), sem("x_variance"), sem("rstd_x_spread")
        s_q, s_sx, s_ft, s_o = sem("gram_turned"), sem("sum_x_done"), sem("feat_turned"), sem("block_out")
        s_zt, s_et, s_h1, s_h2, s_yo = (sem("z_turned"), sem("dense_turned_again"), sem("h1_product"),
                                        sem("h2_product"), sem("y_product"))
        s_yfree = sem("y_row_free")
        a_tr, a_std, a_hi, a_sq, a_sdy, a_z = (sem("embt_copied"), sem("std_s_ready"), sem("u_high"), sem("y_squared"),
                                               sem("std_y_ready"), sem("gram_copied"))
        a_xr, a_dh, a_xs, a_xd = sem("rstd_x_copied"), sem("dense_high"), sem("x_squared"), sem("std_x_ready")
        a_f, a_fh, a_sdo, a_zh, a_eh = (sem("gram_in_feat"), sem("feat_high"), sem("std_o_ready"),
                                        sem("z_high"), sem("dense_high_again"))
        a_h1, a_h2, a_yo = sem("h1_ready"), sem("h2_ready"), sem("y_row_ready")
        a_early = sem("early_moved")
        d_prod, d_var, d_rs, d_sc, d_lo_u = (sem("t_times_s"), sem("var_s_ready"), sem("rstd_s_ready"),
                                             sem("rows_scaled"), sem("u_low"))
        d_vy, d_ry, d_t, d_x = sem("var_y_ready"), sem("rstd_y_ready"), sem("tvec_ready"), sem("x_in_tvec")
        d_dl, d_xr, d_dg, d_xn, d_xt = (sem("dense_low"), sem("rstd_x_ready"), sem("rstd_x_on_diagonal"),
                                        sem("x_normed"), sem("xt_ready"))
        d_f, d_fl, d_zn, d_bn = sem("sum_x_in_feat"), sem("feat_low"), sem("z_ready"), sem("stats_ready")
        d_ag, d_ro, d_zl, d_el = (sem("mean_var_ready"), sem("rstd_o_ready"), sem("z_low"),
                                  sem("dense_low_again"))
        d_h1l = sem("h1_low")

        block = ctx.enter_context(nc.Block())

        def own_block(b, j):
            return b[:, 256 * (j % 2):256 * (j % 2 + 1)].rearrange("t (c j p) -> t c j p", c=2, j=4)[:, :, j, :]

        def gram_place(n, g):
            it, k = divmod(n, 4)
            return 32 * it + 16 * g + 4 * k

        @block.sync
        def _(sp):
            sp.dma_start(ids[:], a["ids"]).then_inc(s_ids, 16)
            sp.dma_start(base[:], a["c_base"]).then_inc(s_ids, 16)
            sp.dma_start(big[:], a["c_big"]).then_inc(s_const, 16)
            sp.dma_start(wsd[:], a["Wsd"]).then_inc(s_const, 16)
            sp.dma_start(small[:], a["small"]).then_inc(s_const, 16)
            sp.dma_start(vecs[:], a["vecs"]).then_inc(s_const, 16)
            sp.dma_start(spread, a["c_spread"]).then_inc(s_const, 16)
            sp.dma_start(bsr[:], a["bs"].to_broadcast([P, E])).then_inc(s_const, 16)

            def load_dense(s):
                sp.dma_start(dense[:], a["dense"][bass.ds(s * P, P), :, :]).then_inc(s_dense, 16)

            def store(b):
                sp.wait_ge(a_yo, b + 2)
                sp.dma_start(out[bass.ds(b, 1), :], yrow[0:1, :]).then_inc(s_out, 16)
                sp.wait_ge(s_out, 16 * b + 16)
                sp.sem_inc(s_yfree, 1)

            load_dense(0)
            sp.dma_start(inds[:], a["c_inds"]).then_inc(s_wl, 16)
            sp.dma_start(w_raw, a["Wl"]).then_inc(s_wl, 16)
            sp.dma_start(w2_raw, a["W2"]).then_inc(s_w2, 16)
            sp.wait_ge(s_dt, 2)
            load_dense(1)
            sp.wait_ge(dw, 2)
            sp.dma_start(w_raw, a["W1"]).then_inc(s_w1, 16)
            with sp.Fori(1, SUPERS - 1) as s:
                sp.wait_ge(s_dt, 2 * s + 2)
                load_dense(s - 1)
                sp.wait_ge(s_et, 2 * s)
                load_dense(s + 1)
                store(s - 1)
            sp.wait_ge(s_dt, 2 * SUPERS)
            load_dense(SUPERS - 2)
            sp.wait_ge(s_et, 2 * SUPERS - 2)
            load_dense(SUPERS - 1)
            store(SUPERS - 2)
            store(SUPERS - 1)

        @block.gpsimd
        def _(pool):
            pool.wait_ge(s_ids, 32)
            nc.gpsimd.tensor_tensor(ids[:].rearrange("p t g i -> p (t g) i"), ids[:].rearrange("p t g i -> p (t g) i"),
                                    base[:].unsqueeze(1).to_broadcast([P, 2 * ITERS * SUPERS, TILES]),
                                    ALU.add).then_inc(s_idx, 1)
            pool.wait_ge(s_idx, 1)
            with pool.Fori(0, SUPERS) as s:
                for it in range(ITERS):
                    b = it % 2
                    nc.gpsimd.tensor_copy(rows_now[it][:], ids[:, bass.ds(ITERS * s + it, 1), :, :].rearrange(
                        "p t g i -> p (t g) i")).then_inc(s_now, 1)
                    pool.wait_ge(s_now, ITERS * s + it + 1)
                    for c, (i0, i1) in enumerate(CHUNKS):
                        pool.wait_ge(d_sc, STEPS * s + 4 * it + c + 1)
                        pool.sem_inc(s_seen, 1)
                        for i in range(i0, i1):
                            for g in range(2):
                                nc.gpsimd.indirect_dma_start(
                                    emb[b][:, i, g, :], None, a["table"],
                                    bass.IndirectOffsetOnAxis(ap=rows_now[it][:, g, i:i + 1], axis=0),
                                ).then_inc(s_row[b][i], 16)

        @block.tensor
        def _(pe):
            def triple(dst, stationary, moving, first, last):
                (sh, sl), (mh, ml) = stationary, moving
                pe.matmul(dst, sh, mh, start=first, stop=False)
                pe.matmul(dst, sh, ml, start=False, stop=False)
                return pe.matmul(dst, sl, mh, start=False, stop=last)

            pe.wait_ge(s_const, 16 * 6)
            pe.matmul(ps_t[:, 0:DS], center, ws, start=True, stop=True)
            for c in range(2):
                pe.matmul(ps_u[:, c * E:(c + 1) * E], wd[:, c * P:(c + 1) * P], center, start=True, stop=True)
            pe.matmul(ps_y[0][0:NF, 0:PJ], wsi, center_p, start=True, stop=True).then_inc(pp, 1)
            pe.wait_ge(dp, 1)
            pe.matmul(ps_t[:, 0:P], wsc2[:].rearrange("p a d -> p (a d)"), wsc2[:].rearrange("p a d -> p (a d)"),
                      start=True, stop=True)
            pe.transpose(ps_u[:, 0:P], wg2[:].rearrange("p a d -> p (a d)"), ident)
            pe.matmul(ps_y[1][:, 0:PJ], ones[0:NF, :], wsit[:], start=True, stop=True).then_inc(pp, 1)
            for i in range(TILES):
                mm = pe.matmul(ps_y[0][:, i * PJ:(i + 1) * PJ], spread[:, i, :], wsit[:], start=True, stop=True)
            mm.then_inc(pp, 1)
            pe.wait_ge(dp, 2)

            def shift_rows(c):
                if c == 0:
                    pe.wait_ge(dw, 1)
                pe.matmul(ps_b[0][0:BM, :], bmat[:, c, :], w_raw[:, c, :], start=(c == 0),
                          stop=(c == FCH - 1)).then_inc(pw, 1)

            def shift_layer1():
                pe.wait_ge(s_w1, 16)
                for m in range(4):
                    for c in range(3):
                        mm = pe.matmul(ps_b[1][:, m:m + 1], w_raw[:, c, m * P:(m + 1) * P], bl[:, c:c + 1],
                                       start=(c == 0), stop=(c == 2))
                mm.then_inc(pw, 1)

            def turn_rows(s, n):
                it, c = divmod(n, 4)
                i0, i1 = CHUNKS[c]
                if after(s, n):
                    pe.wait_ge(d_prod, s * STEPS + n)
                for i in range(i0, i1):
                    pe.wait_ge(s_row[it % 2][i], 64 * s + 32 * (it // 2 + 1))
                    mm = pe.transpose(ps_t[:, (i - i0) * P:(i - i0 + 1) * P],
                                      emb[it % 2][:, i, :, :].rearrange("p g d -> p (g d)"), ident)
                mm.then_inc(s_tr, 1)

            def times_gram(s, n):
                i0, i1 = CHUNKS[n % 4]
                pe.wait_ge(a_tr, s * STEPS + n + 1)
                for i in range(i1 - i0):
                    mm = pe.matmul(ps_t[:, i * P:(i + 1) * P], embt[:, i * P:(i + 1) * P], gram2[:],
                                   start=True, stop=True)
                mm.then_inc(s_t, 1)

            def mix_features(s, n):
                pe.wait_ge(d_sc, s * STEPS + 8 + n + 1)
                if not after(s, n):
                    pe.wait_ge(dp, 3)
                else:
                    pe.wait_ge(a_hi, s * 2 * STEPS + 2 * n)
                    pe.wait_ge(d_lo_u, s * 2 * STEPS + 2 * n)
                k = n % 4
                pieces = u_pieces(k)
                for m, (i, x, y) in enumerate(pieces):
                    f = first_sample(i)
                    mm = pe.matmul(ps_u[:, (x - BS * k) * PJ:(y - BS * k) * PJ],
                                   scaled[:, i, :, :].rearrange("p g d -> p (g d)"),
                                   mix[:, i, x - f:y - f, :].rearrange("p s q -> p (s q)"),
                                   start=(m == 0), stop=(m == len(pieces) - 1), skip_group_check=True)
                mm.then_inc(s_u, 1)

            def project(s, n, g):
                pe.wait_ge(a_hi, s * 2 * STEPS + 2 * n + g + 1)
                pe.wait_ge(d_lo_u, s * 2 * STEPS + 2 * n + g + 1)
                if after(s, n):
                    pe.wait_ge(d_t, s * 2 * STEPS + 2 * n + g - 1)
                pe.matmul(ps_y[g][:, :], wg_hi[:], upair[:, g, :], start=True, stop=False)
                pe.matmul(ps_y[g][:, :], wg_lo[:], ushift[:, g, :], start=False, stop=True).then_inc(s_y, 1)

            def gram_y(s, n, g):
                pe.wait_ge(d_x, s * STEPS + n + 1)
                pe.wait_ge(d_t, s * 2 * STEPS + 2 * n + g + 1)
                if after(s, n + g):
                    pe.wait_ge(a_z, s * 2 * STEPS + 2 * n + g)
                for t in range(4):
                    tv = tvec[:, n % 2, g, t, :]
                    mm = pe.matmul(ps_z[:, t // 2, (t % 2) * TW:(t % 2 + 1) * TW], tv[:, 0:4 * PJ], tv,
                                   start=True, stop=True)
                mm.then_inc(s_z, 1)

            def dense_turn(s, c):
                if c == 0:
                    pe.wait_ge(s_dense, 16 if isinstance(s, int) else 32 * s)
                if c == 0 and not isinstance(s, int):
                    pe.wait_ge(d_f, s)
                if c == 1 and not isinstance(s, int):
                    pe.wait_ge(a_yo, s)
                for j in range(4):
                    mm = pe.transpose(ps_b[1 - c][:, j * P:(j + 1) * P], dense[:, j, c * P:(c + 1) * P], ident)
                mm.then_inc(s_dt, 1)

            def dense_product(s, _):
                pe.wait_ge(d_dl, 2 * s + 2)
                for c in range(2):
                    mm = triple(ps_b[1][:, :], (wd_hi[:, c, :], wd_lo[:, c, :]), (d_hi[:, c, :], d_lo[:, c, :]),
                                c == 0, c == 1)
                mm.then_inc(s_xp, 1)

            def x_sums(s, _):
                pe.wait_ge(a_xs, s + 1)
                for j in range(4):
                    mm = pe.matmul(ps_b[0][:, j:j + 1], xa[:, j * P:(j + 1) * P], ones[:, 0:1], start=True, stop=True)
                mm.then_inc(s_xv, 1)

            def x_spread(s, _):
                pe.wait_ge(d_dg, s + 1)
                pe.matmul(ps_b[0][:, :], ones[:], xa[:], start=True, stop=True).then_inc(s_xs, 1)

            def sum_x(b, _):
                if not isinstance(b, int):
                    pe.wait_ge(a_h2, 2 * b)
                for j in range(4):
                    mm = pe.matmul(ps_b[1][:, j:j + 1], xt[:, j, :], ones[:, 0:1], start=True, stop=True)
                mm.then_inc(s_sx, 1)

            def turn_gram(b, q):
                if q == 0:
                    pe.wait_ge(a_z, 2 * STEPS * (b + 1))
                    pe.wait_ge(a_early, b + 1)
                    if isinstance(b, int):
                        pe.wait_ge(a_yo, b + 1)
                    else:
                        pe.wait_ge(d_xt, b + 2)
                elif q >= 2:
                    pe.wait_ge(a_f, 10 * b + q - 1)
                for m in range(4):
                    mm = pe.transpose(ps_b[q % 2][:, m * P:(m + 1) * P], gram_all[:, 4 * q + m, :], ident)
                mm.then_inc(s_q, 1)

            def turn_feat(b, c):
                if c == 0:
                    pe.wait_ge(a_f, 10 * b + 10)
                    pe.wait_ge(d_f, b + 1)
                if c < 2:
                    pe.wait_ge(d_el, 2 * b + c + 1)
                else:
                    pe.wait_ge(d_fl, FCH * b + c - 1)
                for j in range(4):
                    mm = pe.transpose(ps_b[c % 2][:, j * P:(j + 1) * P], feat[:, j, c * P:(c + 1) * P], ident)
                mm.then_inc(s_ft, 1)

            def products(dst, count, first, last, operands, done):
                for at in range(first, last):
                    c, i = divmod(at, 3)
                    mm = pe.matmul(dst, *operands(c, i), start=(at == 0), stop=(at == count - 1))
                if last == count:
                    mm.then_inc(done, 1)

            def linear(b, j, first, last):
                if first == 0:
                    if j == 0:
                        pe.wait_ge(d_fl, FCH * b + 4)
                    elif j == 1:
                        pe.wait_ge(d_fl, FCH * b + FCH)
                    else:
                        pe.wait_ge(d_zn, 4 * b + j - 1)
                if first <= 12 < last:
                    pe.wait_ge(d_fl, FCH * b + FCH)
                r = slice(j * P, (j + 1) * P)
                products(ps_b[1 - j % 2][:, :], 15, first, last,
                         lambda c, i: ((f_hi, f_hi, f_lo)[i][:, c, r], (wl_hi, wl_lo, wl_hi)[i][:, c, :]), s_o)

            def turn_dense(b, c):
                if c == 0:
                    pe.wait_ge(s_dense, 32 * b + 48 if not isinstance(b, int) else 32 * SUPERS)
                pe.wait_ge(a_f, 10 * b + 9 + c)
                for j in range(4):
                    mm = pe.transpose(ps_b[c][:, j * P:(j + 1) * P], dense[:, j, c * P:(c + 1) * P], ident)
                mm.then_inc(s_et, 1)

            def turn_z(b, c):
                if c == 0:
                    pe.wait_ge(d_zn, 4 * b + 4)
                if c == 2:
                    pe.wait_ge(d_zl, 3 * b + 1)
                for j in range(4):
                    mm = pe.transpose(ps_b[1 - c % 2][:, j * P:(j + 1) * P], zn[:, j, c * P:(c + 1) * P], ident)
                mm.then_inc(s_zt, 1)

            def layer1(b, m, first, last):
                if first == 0:
                    if m == 0:
                        pe.wait_ge(d_zl, 3 * b + 2)
                    elif m == 1:
                        pe.wait_ge(d_zl, 3 * b + 3)
                    else:
                        pe.wait_ge(a_h1, 4 * b + m - 1)
                if first <= 12 < last:
                    pe.wait_ge(d_zl, 3 * b + 3)
                r = slice(m * P, (m + 1) * P)
                products(ps_b[m % 2][:, :], 15, first, last,
                         lambda c, i: ((w1_hi, w1_hi, w1_lo)[i][:, (c + 3) % 5, r],
                                       (d_hi, d_lo, d_hi)[i][:, c, :] if c < 2 else (z_hi, z_lo, z_hi)[i][:, c - 2, :]),
                         s_h1)

            def layer2(b, m, first, last):
                if first == 0:
                    pe.wait_ge(a_h1, 4 * b + 3 + m)
                if m == 0:
                    pe.wait_ge(d_h1l, 4 * b + min(4, (last - 1) // 3 + 1))
                r = slice(m * P, (m + 1) * P)
                products(ps_b[m][:, :], 12, first, last,
                         lambda c, i: ((w2_hi, w2_hi, w2_lo)[i][:, c, r], (h1_hi, h1_lo, h1_hi)[i][:, c, :]), s_h2)

            def layer3(b, _):
                for m in range(2):
                    pe.wait_ge(a_h2, 2 * b + m + 1)
                    mm = pe.matmul(ps_b[0][0:1, :], w3[:, m:m + 1], h2[:, m, :], start=(m == 0), stop=(m == 1))
                mm.then_inc(s_yo, 1)

            stage = {"dense_turn": dense_turn, "dense_product": dense_product, "x_sums": x_sums, "x_spread": x_spread,
                     "sum_x": sum_x, "turn_gram": turn_gram, "turn_feat": turn_feat, "linear": linear,
                     "turn_z": turn_z, "turn_dense": turn_dense, "layer1": layer1, "layer2": layer2, "layer3": layer3}

            def steps(s, b, count=STEPS):
                front = s if not isinstance(s, int) or s < SUPERS else None
                for n in range(count):
                    now, last, older = back_to(s, n), back_to(s, n - 1), back_to(s, n - 2)
                    if now:
                        turn_rows(*now)
                    if last:
                        mix_features(*last)
                    run_slot(stage, SLOTS, 2 * n, front, b)
                    if now:
                        times_gram(*now)
                    if older:
                        gram_y(*older, 0)
                    if b is None and n == 3:
                        shift_rows(0)
                    if b is None and 3 <= n <= 6:
                        shift_rows(n - 2)
                    if b is None and n == 12:
                        shift_layer1()
                    if last:
                        project(*last, 0)
                    run_slot(stage, SLOTS, 2 * n + 1, front, b)
                    if last:
                        project(*last, 1)
                    if older:
                        gram_y(*older, 1)

            steps(0, None)
            pe.wait_ge(dw, 3)
            sum_x(0, 0)
            with pe.Fori(1, SUPERS) as s:
                steps(s, s - 1)
            steps(SUPERS, SUPERS - 1)

        @block.scalar
        def _(act):
            def copy_turned(s, n):
                i0, i1 = CHUNKS[n % 4]
                w = (i1 - i0) * P
                act.wait_ge(s_tr, s * STEPS + n + 1)
                nc.scalar.activation(embt[:, 0:w], ps_t[:, 0:w], ACT.Copy).then_inc(a_tr, 1)

            def root_s(s, n):
                i0, i1 = CHUNKS[n % 4]
                w = 2 * (i1 - i0)
                act.wait_ge(d_var, s * STEPS + n + 1)
                nc.scalar.activation(std_s[:, 0:w], var_s[:, 0:w], ACT.Sqrt, bias=eps[:, 0:1],
                                     scale=1.0 / E).then_inc(a_std, 1)

            def u_high(s, n, g):
                act.wait_ge(s_u, s * STEPS + n + 1)
                nc.scalar.activation(upair[0:DS, g, :], ps_u[DS * g:DS * g + DS, :], ACT.Copy)
                nc.scalar.activation(ushift[0:DS, g, :], ps_u[DS * g:DS * g + DS, :], ACT.Copy).then_inc(a_hi, 1)

            def square_y(s, n, g):
                act.wait_ge(s_y, s * 2 * STEPS + 2 * n + g + 1)
                if after(s, n):
                    act.wait_ge(d_vy, s * 2 * STEPS + 2 * n + g - 1)
                nc.scalar.activation(ysq[:, g, :], ps_y[g][:, :], ACT.Square).then_inc(a_sq, 1)

            def root_y(s, n, g):
                act.wait_ge(d_vy, s * 2 * STEPS + 2 * n + g + 1)
                nc.scalar.activation(std_y[:, g, :], var_y[:, g, :], ACT.Sqrt, bias=eps[:, 0:1],
                                     scale=1.0 / PJ).then_inc(a_sdy, 1)

            def copy_gram(s, n, g):
                act.wait_ge(s_z, s * 2 * STEPS + 2 * n + g + 1)
                if n == EARLY and g == 0 and not isinstance(s, int):
                    act.wait_ge(s_q, (NG + 2) * s)
                if n < EARLY:
                    dst = gram_early[:, :, g, 4 * n:4 * n + 4]
                else:
                    dst = gram_all[:, :, gram_place(n, g):gram_place(n, g) + 4]
                src = ps_z[:, :, 0:2 * TW].rearrange("p b (t q) -> p b t q", t=2)
                for j in range(4):
                    r = slice(32 * j, 32 * j + 32)
                    nc.scalar.activation(dst[r, 0:PJ, :].rearrange("p q (b t) -> p b t q", b=2),
                                         src[r, :, :, PJ * j:PJ * (j + 1)], ACT.Copy)
                nc.scalar.activation(dst[:, PJ:PJ + 8, :].rearrange("p q (b t) -> p b t q", b=2),
                                     src[:, :, :, 4 * PJ:TW], ACT.Copy).then_inc(a_z, 1)

            def dense_turn(s, c):
                act.wait_ge(s_dt, 2 * s + c + 1)
                nc.scalar.activation(d_hi[:, c, :], ps_b[1 - c][:, :], ACT.Copy).then_inc(a_dh, 1)

            def dense_product(s, _):
                act.wait_ge(s_xp, s + 1)
                nc.scalar.activation(xa[:], ps_b[1][:, :], ACT.Square).then_inc(a_xs, 1)

            def x_sums(s, _):
                act.wait_ge(s_xv, s + 1)
                nc.scalar.activation(std_x[:], ps_b[0][:, 0:4], ACT.Sqrt, bias=eps[:, 0:1],
                                     scale=1.0 / E).then_inc(a_xd, 1)

            def x_spread(s, _):
                act.wait_ge(s_xs, s + 1)
                nc.scalar.activation(xb[:], ps_b[0][:, :], ACT.Copy).then_inc(a_xr, 1)

            def move_early(s):
                act.wait_ge(a_z, 2 * STEPS * s + 2 * EARLY)
                nc.scalar.activation(gram_all[:, :, 0:32].rearrange("p q (g t) -> p q g t", g=2)[:, :, :, 0:4 * EARLY],
                                     gram_early[:], ACT.Copy).then_inc(a_early, 1)

            def turn_gram(b, q):
                act.wait_ge(s_q, (NG + 2) * b + q + 1)
                src = ps_b[q % 2]
                if q < NG:
                    w = 4 * q + 3
                    dst = feat[:, :, OFF[q]:OFF[q] + 4 * w].rearrange("t j (m p) -> t m j p", m=4)
                    src = src[:, :].rearrange("t (m j p) -> t m j p", m=4, j=4)[:, :, :, 0:w]
                    last = nc.scalar.activation(dst, src, ACT.Copy)
                else:
                    for j in range(2 * (q - NG), 2 * (q - NG) + 2):
                        last = nc.scalar.activation(feat[:, j, XOFF:XOFF + 2 * PJ].rearrange("t (c p) -> t c p", c=2),
                                                    own_block(src, j), ACT.Copy)
                last.then_inc(a_f, 1)

            def turn_feat(b, c):
                act.wait_ge(s_ft, FCH * b + c + 1)
                nc.scalar.activation(f_hi[:, c, :], ps_b[c % 2][:, :], ACT.Copy).then_inc(a_fh, 1)

            def linear_root(b, j):
                act.wait_ge(d_ag, 4 * b + j + 1)
                nc.scalar.activation(std_o[:, j:j + 1], mv[:, j, 1:2], ACT.Sqrt, bias=eps[:, 0:1]).then_inc(a_sdo, 1)

            def turn_z(b, c):
                act.wait_ge(s_zt, 3 * b + c + 1)
                nc.scalar.activation(z_hi[:, c, :], ps_b[1 - c % 2][:, :], ACT.Copy).then_inc(a_zh, 1)

            def turn_dense(b, c):
                act.wait_ge(s_et, 2 * b + c + 1)
                nc.scalar.activation(d_hi[:, c, :], ps_b[c][:, :], ACT.Copy).then_inc(a_eh, 1)

            def layer1(b, m):
                act.wait_ge(s_h1, 4 * b + m + 1)
                nc.scalar.activation(h1_hi[:, m, :], ps_b[m % 2][:, :], ACT.Relu, bias=b1z[:, m:m + 1])
                nc.scalar.activation(h1f[m], ps_b[m % 2][:, :], ACT.Relu, bias=b1z[:, m:m + 1]).then_inc(a_h1, 1)

            def layer2(b, m):
                act.wait_ge(s_h2, 2 * b + m + 1)
                nc.scalar.activation(h2[:, m, :], ps_b[m][:, :], ACT.Relu, bias=b2[:, m:m + 1]).then_inc(a_h2, 1)

            def layer3(b, _):
                act.wait_ge(s_yo, b + 1)
                act.wait_ge(s_yfree, b + 1)
                nc.scalar.activation(yrow[0:1, :].rearrange("o (t j) -> o t j", j=4),
                                     ps_b[0][0:1, :].rearrange("o (j t) -> o t j", j=4), ACT.Copy).then_inc(a_yo, 1)

            slots = readers({"dense_turn": ("dense_turn", 0), "dense_product": ("dense_product", 0),
                             "x_sums": ("x_sums", 0), "x_spread": ("x_spread", 0), "turn_gram": ("turn_gram", 0),
                             "turn_feat": ("turn_feat", 0),
                             "linear_root": ("linear", 1), "turn_z": ("turn_z", 0),
                             "turn_dense": ("turn_dense", 0), "layer1": ("layer1", 0), "layer2": ("layer2", 0),
                             "layer3": ("layer3", 0)})
            slots[14].insert(0, ("move_early",))
            stage = {"dense_turn": dense_turn, "dense_product": dense_product, "x_sums": x_sums,
                     "x_spread": x_spread, "move_early": move_early,
                     "turn_gram": turn_gram, "turn_feat": turn_feat, "linear_root": linear_root,
                     "turn_z": turn_z,
                     "turn_dense": turn_dense, "layer1": layer1, "layer2": layer2, "layer3": layer3}

            def steps(s, b, count=STEPS):
                front = s if not isinstance(s, int) or s < SUPERS else None
                for n in range(count):
                    now, last, older = back_to(s, n), back_to(s, n - 1), back_to(s, n - 2)
                    if now:
                        copy_turned(*now)
                    if older:
                        root_y(*older, 1)
                    if last:
                        u_high(*last, 0)
                        u_high(*last, 1)
                    run_slot(stage, slots, 2 * n, front, b)
                    if older:
                        copy_gram(*older, 0)
                    if now:
                        root_s(*now)
                    run_slot(stage, slots, 2 * n + 1, front, b)
                    if last:
                        square_y(*last, 0)
                        square_y(*last, 1)
                        root_y(*last, 0)
                    if older:
                        copy_gram(*older, 1)
                    if b is None:
                        weights(n)

            def weights_scale(row, scale, count):
                nc.scalar.activation(row, row, ACT.Copy, scale=scale).then_inc(aw, 1)
                act.wait_ge(aw, count)

            def weights_high(hi, src):
                nc.scalar.activation(hi, src, ACT.Copy).then_inc(a_wh, 1)

            def weights(n):
                if 3 <= n <= 7:
                    c = n - 3
                    act.wait_ge(pw, c + 1)
                    weights_scale(w_raw[:, c, :], ga[:, c:c + 1], c + 1)
                if 5 <= n <= 9:
                    c = n - 5
                    act.wait_ge(d_wc, c + 1)
                    weights_high(wl_hi[:, c, :], w_raw[:, c, :])
                if n == 10:
                    act.wait_ge(s_w2, 16)
                    weights_high(w2_hi[:], w2_raw)
                for c in {12: (0,), 13: (1,), 14: (2, 3), 15: (4,)}.get(n, ()):
                    act.wait_ge(pw, FCH + 1)
                    if c < 3:
                        weights_scale(w_raw[:, c, :], gl[:, c:c + 1], FCH + 1 + c)
                    weights_high(w1_hi[:, c, :], w_raw[:, c, :])

            act.sem_inc(a_yo, 1)
            act.sem_inc(s_yfree, 1)
            act.wait_ge(dp, 2)
            steps(0, None)
            with act.Fori(1, SUPERS) as s:
                steps(s, s - 1)
            steps(SUPERS, SUPERS - 1)

        @block.vector
        def _(dve):
            V = nc.vector
            chain = [0]

            def link(ins):
                chain[0] += 1
                ins.then_inc(s_chain, 1)
                dve.wait_ge(s_chain, chain[0])

            def pair(hi, lo, src):
                link(V.tensor_copy(hi, src))
                return V.tensor_tensor(lo, src, hi.bitcast(F32), ALU.subtract)

            dve.sem_inc(d_sc, 8)
            V.memset(ones[:], 1.0).then_inc(s_chain, 1)
            V.memset(eps[:], EPS).then_inc(s_chain, 1)
            V.memset(tvec[:], 1.0).then_inc(s_chain, 1)
            chain[0] = 3
            dve.wait_ge(s_const, 16 * 6)
            dve.wait_ge(pp, 1)
            for g in range(2):
                link(V.tensor_copy(wsc2[:, g, :], ps_t[:, 0:DS]))
            link(V.tensor_scalar(wg2[:], wsc2[:], gs[:, 0:1], None, ALU.mult))
            link(V.tensor_copy(wd_hi[:].rearrange("p c e -> p (c e)"), ps_u[:, 0:DD]))
            link(V.tensor_tensor(wd_lo[:].rearrange("p c e -> p (c e)"), ps_u[:, 0:DD],
                                 wd_hi[:].rearrange("p c e -> p (c e)").bitcast(F32), ALU.subtract))
            V.tensor_copy(wsit[:], ps_y[0][0:NF, 0:PJ]).then_inc(dp, 1)
            dve.wait_ge(pp, 2)
            link(V.tensor_tensor(gram2[:], ps_t[:, 0:P], blockmask, ALU.mult))
            V.memset(var_s[:], 0.0).then_inc(dp, 1)
            link(V.tensor_copy(wg_hi[:], ps_u[:, 0:P]))
            H = slice(DS, P)
            link(V.tensor_tensor(wg_lo[0:DS], ps_u[0:DS, 0:P], wg_hi[0:DS].bitcast(F32), ALU.subtract))
            split(link, V, shift_t[H, 0, :], wg_lo[H], bsr[H, :], shift_t[H, 1, :], shift_t[H, 2, :],
                  rowmask[H, 0:1], rowmask[H, 1:2])
            link(V.tensor_copy(shift_t[H, 0, 0:PJ], ps_y[1][H, 0:PJ]))
            split(link, V, shift_t[H, 0, 0:PJ], ushift[H, 0, 0:PJ], shift_t[H, 0, 0:PJ], shift_t[H, 1, 0:PJ],
                  shift_t[H, 2, 0:PJ], rowmask[H, 2:3], rowmask[H, 3:4])
            link(V.tensor_copy(shift_t[H, 0, 0:PJ], ushift[H, 0, 0:PJ].bitcast(F32)))
            for g in range(2):
                link(V.tensor_copy(ushift[H, g, :].rearrange("p (s q) -> p s q", q=PJ),
                                   shift_t[H, 0, 0:PJ].unsqueeze(1).to_broadcast([DS, BS, PJ])))
            dve.wait_ge(pp, 3)
            for w in range(WINDOW):
                ins = V.tensor_tensor(mix[:, :, w, :], ps_y[0][:, 0:TILES * PJ].rearrange("p (i q) -> p i q", q=PJ),
                                      window[:, :, w:w + 1].to_broadcast([P, TILES, PJ]), ALU.mult)
                ins.then_inc(s_chain, 1)
            chain[0] += WINDOW
            dve.wait_ge(s_chain, chain[0])
            V.memset(var_s[:], 0.0).then_inc(dp, 1)

            def shift_matrix():
                dve.wait_ge(s_wl, 32)
                lo = ROFF - 4 * P
                link(V.tensor_tensor(ga, ga, gb, ALU.mult))
                V.memset(bmat, 0.0).then_inc(s_chain, 1)
                V.tensor_tensor(ind_p, ind_p, bb.unsqueeze(2).to_broadcast([P, FCH, QC]), ALU.mult).then_inc(s_chain, 1)
                chain[0] += 2
                link(V.tensor_tensor(ind_q, ind_q, ba.unsqueeze(2).to_broadcast([P, FCH, QC]), ALU.mult))
                link(V.tensor_tensor(bmat[:, :, lo:lo + QC], ind_p, ind_q, ALU.add))
                V.scalar_tensor_tensor(bmat[:, :, lo + QC - 1:lo + QC].rearrange("p c o -> p (c o)"), ba, float(E), bb,
                                       ALU.mult, ALU.mult).then_inc(dw, 1)

            def weights_linear(c):
                dve.wait_ge(aw, c + 1)
                row = w_raw[:, c, :]
                if c == FCH - 1:
                    link(V.scalar_tensor_tensor(row[0:BM], ps_b[0][0:BM, :], gr[0:BM, 0:1], row[0:BM],
                                                ALU.mult, ALU.add))
                link(V.tensor_reduce(std_o[:, 0:1], row, AX.X, ALU.add))
                link(V.tensor_scalar(std_o[:, 1:2], std_o[:, 0:1], -1.0 / KOUT, None, ALU.mult))
                V.tensor_scalar(row, row, std_o[:, 1:2], None, ALU.add).then_inc(d_wc, 1)

            def weights_low(done, lo, src, hi):
                dve.wait_ge(a_wh, done)
                return V.tensor_tensor(lo, src, hi.bitcast(F32), ALU.subtract)

            def u_low(s, n, g):
                dve.wait_ge(a_hi, s * 2 * STEPS + 2 * n + g + 1)
                V.tensor_tensor(upair[DS:P, g, :], ps_u[DS * g:DS * g + DS, :],
                                upair[0:DS, g, :].bitcast(F32), ALU.subtract).then_inc(d_lo_u, 1)

            def variance_s(s, n):
                it, c = divmod(n, 4)
                i0, i1 = CHUNKS[c]
                w = 2 * (i1 - i0)
                dve.wait_ge(s_t, s * STEPS + n + 1)
                V.tensor_tensor(prod[:, 0:w, :], ps_t[:, 0:w * DS].rearrange("p (w d) -> p w d", d=DS),
                                emb[it % 2][:, i0:i1, :, :].rearrange("p i g d -> p (i g) d"),
                                ALU.mult).then_inc(d_prod, 1)
                dve.wait_ge(d_prod, s * STEPS + n + 1)
                V.tensor_reduce(var_s[:, 0:w], prod[:, 0:w, :], AX.X, ALU.add).then_inc(d_var, 1)

            def scale_s(s, n):
                it, c = divmod(n, 4)
                i0, i1 = CHUNKS[c]
                w = 2 * (i1 - i0)
                dve.wait_ge(a_std, s * STEPS + n + 1)
                V.reciprocal(rstd_s[:, 0:w], std_s[:, 0:w]).then_inc(d_rs, 1)
                dve.wait_ge(d_rs, s * STEPS + n + 1)
                V.tensor_tensor(scaled[:, i0:i1, :, :].rearrange("p i g d -> p (i g) d"),
                                emb[it % 2][:, i0:i1, :, :].rearrange("p i g d -> p (i g) d"),
                                rstd_s[:, 0:w].unsqueeze(2).to_broadcast([P, w, DS]), ALU.mult).then_inc(d_sc, 1)

            def variance_y(s, n, g):
                dve.wait_ge(a_sq, s * 2 * STEPS + 2 * n + g + 1)
                V.tensor_reduce(var_y[:, g, :], ysq[:, g, :].rearrange("p (s q) -> p s q", q=PJ), AX.X,
                                ALU.add).then_inc(d_vy, 1)

            def norm_y(s, n, g):
                dve.wait_ge(a_sdy, s * 2 * STEPS + 2 * n + g + 1)
                V.reciprocal(rstd_y[:, g, :], std_y[:, g, :]).then_inc(d_ry, 1)
                dve.wait_ge(d_ry, s * 2 * STEPS + 2 * n + g + 1)
                V.tensor_tensor(tvec[:, n % 2, g, :, 0:4 * PJ].rearrange("p t (j q) -> p t j q", j=4),
                                ps_y[g][:, :].rearrange("p (t j q) -> p t j q", t=4, j=4),
                                rstd_y[:, g, :].rearrange("p (t j) -> p t j", t=4).unsqueeze(3).to_broadcast(
                                    [P, 4, 4, PJ]), ALU.mult).then_inc(d_t, 1)

            def x_column(s, n):
                if n == 0:
                    dve.wait_ge(d_xt, s + 1)
                if after(s, n, 2):
                    dve.wait_ge(s_z, s * 2 * STEPS + 2 * n - 2)
                for g in range(2):
                    t0 = gram_place(n, g)
                    last = V.tensor_copy(tvec[:, n % 2, g, :, 4 * PJ:TW:2],
                                         xt[:, :, t0:t0 + 4].rearrange("p j t -> p t j"))
                last.then_inc(d_x, 1)

            def dense_turn(s, c):
                dve.wait_ge(a_dh, 2 * s + c + 1)
                V.tensor_tensor(d_lo[:, c, :], ps_b[1 - c][:, :], d_hi[:, c, :].bitcast(F32),
                                ALU.subtract).then_inc(d_dl, 1)

            def x_sums(s, _):
                dve.wait_ge(a_xd, s + 1)
                V.reciprocal(rstd_x[:], std_x[:]).then_inc(d_xr, 1)
                dve.wait_ge(d_xr, s + 1)
                V.tensor_tensor(xa[:].rearrange("p (j t) -> p j t", j=4), ident.unsqueeze(1).to_broadcast([P, 4, P]),
                                rstd_x[:].unsqueeze(2).to_broadcast([P, 4, P]), ALU.mult).then_inc(d_dg, 1)

            def x_spread(s, _):
                dve.wait_ge(a_xr, s + 1)
                V.tensor_tensor(xb[:], ps_b[1][:, :], xb[:], ALU.mult).then_inc(d_xn, 1)
                dve.wait_ge(d_xn, s + 1)
                V.tensor_scalar(xt[:].rearrange("p j t -> p (j t)"), xb[:], gd[:, 0:1], bd[:, 0:1],
                                ALU.mult, ALU.add).then_inc(d_xt, 1)

            def sum_x(b, _):
                dve.wait_ge(s_sx, b + 1)
                V.tensor_copy(feat[:, :, SXOFF:SXOFF + 1].rearrange("t j o -> t (j o)"),
                              ps_b[1][:, 0:4]).then_inc(d_f, 1)

            def turn_feat(b, c):
                dve.wait_ge(a_fh, FCH * b + c + 1)
                V.tensor_tensor(f_lo[:, c, :], ps_b[c % 2][:, :], f_hi[:, c, :].bitcast(F32),
                                ALU.subtract).then_inc(d_fl, 1)

            def linear(b, j):
                dve.wait_ge(s_o, 4 * b + j + 1)
                V.bn_stats(stats[:, j, :], ps_b[1 - j % 2][:, :]).then_inc(d_bn, 1)
                dve.wait_ge(d_bn, 4 * b + j + 1)
                dve.sem_inc(s_seen, 1)
                V.bn_aggr(mv[:, j, :], stats[:, j, :]).then_inc(d_ag, 1)

            def linear_out(b, j):
                dve.wait_ge(a_sdo, 4 * b + j + 1)
                V.reciprocal(rstd_o[:, j:j + 1], std_o[:, j:j + 1]).then_inc(d_ro, 1)
                dve.wait_ge(d_ro, 4 * b + j + 1)
                V.tensor_scalar(zn[:, j, :], ps_b[1 - j % 2][:, 0:KUSE], rstd_o[:, j:j + 1], None,
                                ALU.mult).then_inc(d_zn, 1)

            def turn_z(b, c):
                dve.wait_ge(a_zh, 3 * b + c + 1)
                V.tensor_tensor(z_lo[:, c, :], ps_b[1 - c % 2][:, :], z_hi[:, c, :].bitcast(F32),
                                ALU.subtract).then_inc(d_zl, 1)

            def turn_dense(b, c):
                dve.wait_ge(a_eh, 2 * b + c + 1)
                V.tensor_tensor(d_lo[:, c, :], ps_b[c][:, :], d_hi[:, c, :].bitcast(F32),
                                ALU.subtract).then_inc(d_el, 1)

            def layer1(b, m):
                dve.wait_ge(a_h1, 4 * b + m + 1)
                V.tensor_tensor(h1_lo[:, m, :], h1f[m], h1_hi[:, m, :].bitcast(F32), ALU.subtract).then_inc(d_h1l, 1)

            slots = readers({"dense_turn": ("dense_turn", 0), "x_sums": ("x_sums", 0), "x_spread": ("x_spread", 0),
                             "sum_x": ("sum_x", 0), "turn_feat": ("turn_feat", 0), "linear": ("linear", 0),
                             "linear_out": ("linear", 1), "turn_z": ("turn_z", 0),
                             "turn_dense": ("turn_dense", 0), "layer1": ("layer1", 0)})
            stage = {"dense_turn": dense_turn, "x_sums": x_sums, "x_spread": x_spread,
                     "sum_x": sum_x, "turn_feat": turn_feat, "linear": linear, "linear_out": linear_out,
                     "turn_z": turn_z, "turn_dense": turn_dense, "layer1": layer1}

            def steps(s, b, count=STEPS):
                front = s if not isinstance(s, int) or s < SUPERS else None
                for n in range(count):
                    now, last = back_to(s, n), back_to(s, n - 1)
                    if last:
                        u_low(*last, 0)
                    run_slot(stage, slots, 2 * n, front, b)
                    if now:
                        variance_s(*now)
                    if last:
                        u_low(*last, 1)
                    if now:
                        scale_s(*now)
                    if last:
                        variance_y(*last, 0)
                        variance_y(*last, 1)
                    run_slot(stage, slots, 2 * n + 1, front, b)
                    if b is None:
                        if n == 2:
                            shift_matrix()
                        if 4 <= n <= 8:
                            weights_linear(n - 4)
                        if 6 <= n <= 10:
                            low = weights_low(n - 5, wl_lo[:, n - 6, :], w_raw[:, n - 6, :], wl_hi[:, n - 6, :])
                            if n == 10:
                                low.then_inc(dw, 1)
                        if n == 11:
                            link(weights_low(FCH + 1, w2_lo[:], w2_raw, w2_hi[:]))
                        if n == 12:
                            dve.wait_ge(pw, FCH + 1)
                            link(V.tensor_tensor(b1z[:], ps_b[1][:, 0:4], b1, ALU.add))
                        for c in {13: (0,), 14: (1, 2), 15: (3, 4)}.get(n, ()):
                            link(weights_low(FCH + 2 + c, w1_lo[:, c, :], w_raw[:, c, :], w1_hi[:, c, :]))
                        if n == 15:
                            link(V.memset(feat[:, :, ONEOFF:FEAT], 0.0))
                            V.memset(feat[:, :, ONEOFF:ONEOFF + 1], 1.0).then_inc(dw, 1)
                    if last:
                        x_column(*last)
                        norm_y(*last, 0)
                        norm_y(*last, 1)

            steps(0, None)
            sum_x(0, 0)
            with dve.Fori(1, SUPERS) as s:
                steps(s, s - 1)
            steps(SUPERS, SUPERS - 1)


def split(link, V, tmp, dst, src, hi, lo, take_hi, take_lo):
    link(V.tensor_copy(dst, src))
    link(V.tensor_copy(hi, dst.bitcast(F32)))
    link(V.tensor_tensor(lo, src, hi, ALU.subtract))
    link(V.tensor_scalar(hi, hi, take_hi, None, ALU.mult))
    link(V.scalar_tensor_tensor(dst, lo, take_lo, hi, ALU.mult, ALU.add))


def constants():
    r = np.arange(P)
    c = {}
    row = P * np.arange(TILES)[None, :] + r[:, None]
    c["c_spread"] = (np.arange(NF)[:, None, None] == (row % NF).T[None])
    first = np.array([first_sample(i) for i in range(TILES)])
    window = (row // NF - first)[:, :, None] == np.arange(WINDOW)
    c["c_big"] = np.concatenate([np.eye(P), np.eye(P) - 1.0 / E, np.kron(np.eye(2), np.ones((DS, DS))),
                                 window.reshape(P, -1)], axis=1)
    p, q, col = feature_map()
    ip, iq = np.zeros((FEAT, QC)), np.zeros((FEAT, QC))
    for f in range(FEAT):
        if q[f] >= 0:
            ip[f, p[f]] = 1
            iq[f, q[f]] = 1
        elif p[f] >= 0:
            iq[f, PJ] = 1
    c["c_inds"] = np.stack([ip, iq]).reshape(2, FCH, P, QC).transpose(2, 0, 1, 3)
    return {k: np.ascontiguousarray(v, dtype=np.float32) for k, v in c.items()}


def feature_map():
    p, q, col = (np.full(FEAT, -1) for _ in range(3))
    for g in range(NG):
        w = 4 * g + 3
        for m in range(4):
            for x in range(w):
                y = 4 * g + m
                if x < y:
                    f = OFF[g] + m * w + x
                    p[f], q[f], col[f] = x, y, (y + 1) * y // 2 + x + 1
    for x in range(PJ):
        p[XOFF + x], col[XOFF + x] = x, (x + 1) * x // 2
    return p, q, col


def kernel(**inputs):
    import concourse.bacc as _bacc
    from concourse.bass_utils import run_bass_kernel_spmd as _run

    x = {k: np.asarray(v) for k, v in inputs.items()}
    table = np.concatenate([x[f"tbl_{f}"] for f in range(NF)], axis=0)
    begin = np.cumsum([0] + [x[f"tbl_{f}"].shape[0] for f in range(NF - 1)])
    row = P * np.arange(TILES)[None, :] + np.arange(P)[:, None]
    p, q, col = feature_map()

    def place(v, where, none):
        full = np.full((FEAT,) + v.shape[1:], none, np.float32)
        full[where >= 0] = v[where[where >= 0]]
        return np.ascontiguousarray(full.reshape((FCH, P) + v.shape[1:]).swapaxes(0, 1))

    def cols(v, n):
        return np.ascontiguousarray(v.reshape(n, P).T)

    gsi, bsi = x["L0_rec_gsi"], x["L0_rec_bsi"]
    gr = np.zeros((P, 1), np.float32)
    gr[ROFF - 4 * P:ROFF - 4 * P + PJ, 0] = gsi
    gr[SXOFF - 4 * P:ONEOFF - 4 * P + 1, 0] = 1.0
    rowmask = np.zeros((P, 4), np.float32)
    rowmask[DS:DS + 4] = [[1, 0, 1, 0], [1, 0, 0, 1], [0, 1, 1, 0], [0, 1, 0, 1]]
    vectors = {"gs": x["L0_rec_gs"].reshape(P, 1), "gd": x["L0_rec_gd"].reshape(P, 1),
               "bd": x["L0_rec_bd"].reshape(P, 1), "gr": gr, "ga": place(gsi, p, 1.0), "gb": place(gsi, q, 1.0),
               "ba": place(bsi, p, 0.0), "bb": place(bsi, q, 0.0), "gl": cols(x["L0_rec_gl"][:KUSE], 3),
               "bl": cols(x["L0_rec_bl"][:KUSE], 3), "b1": cols(x["b_top1"], 4), "b2": cols(x["b_top2"], 2),
               "w3": cols(x["W_top3"], 2), "rowmask": rowmask}
    w1 = x["W_top1"].reshape(6, P, H1)
    arrays = {
        "table": table,
        "ids": np.ascontiguousarray(x["ids"].reshape(-1, P).T).reshape(P, ITERS * SUPERS, 2, TILES),
        "c_base": np.ascontiguousarray(begin[row % NF].astype(np.int32)),
        "dense": np.ascontiguousarray(x["r_dense_t"]).reshape(SUPERS * P, 4, DD),
        "Wsd": np.concatenate([x["L0_rec_Ws"], x["L0_rec_Wd"]], axis=1),
        "small": np.concatenate([(np.eye(PJ) - 1.0 / PJ).astype(np.float32), x["L0_rec_Wsi"]], axis=1),
        "bs": x["L0_rec_bs"].reshape(1, P),
        "vecs": np.concatenate([vectors[name] for name in VECS], axis=1),
        "Wl": place(x["L0_rec_Wl"].T, col, 0.0),
        "W1": np.ascontiguousarray(w1[[0, 1, 2, 4, 5]].transpose(1, 0, 2)),
        "W2": np.ascontiguousarray(x["W_top2"].reshape(4, P, H2).transpose(1, 0, 2)),
        **constants(),
    }
    nc = _bacc.Bacc("TRN2", target_bir_lowering=False, num_devices=1)
    a, feed = {}, {}
    for name, v in arrays.items():
        v = np.ascontiguousarray(v)
        feed[f"in_{name}"] = v
        a[name] = nc.dram_tensor(f"in_{name}", v.shape, mybir.dt.from_np(v.dtype), kind="ExternalInput").ap()
    out = nc.dram_tensor("out_y", (SUPERS, SUPER), F32, kind="ExternalOutput").ap()
    build(nc, a, out)
    r = _run(nc, [feed], core_ids=[0])
    return r.results[0]["out_y"].reshape(BATCH, 1)
```
